# Optimizing a Trainium2 kernel written in Bass

```python
import numpy as np
import jax
import jax.numpy as jnp

def _softmax(x, axis=-1):
    return jax.nn.softmax(x, axis=axis)

def _gelu(x):
    return jax.nn.gelu(x, approximate=True)

def _silu(x):
    return jax.nn.silu(x)

def _sigmoid(x):
    return jax.nn.sigmoid(x)

def _layernorm(x, axis=-1, eps=1e-05):
    m = jnp.mean(x, axis=axis, keepdims=True)
    v = jnp.var(x, axis=axis, keepdims=True)
    return (x - m) / jnp.sqrt(v + eps)

def _scatter_add(tgt, idx, src, axis=0):
    return tgt.at[idx].add(src)

def _segment_sum(src, seg, n):
    return jax.ops.segment_sum(src, seg, n)
kernel_name = 'mk_sandwich_d1_jaxref_r8_0d89ff'

def setup_inputs(seed: int=0):
    np.random.seed(seed)
    _w = jnp.asarray

    def _L0_attn_setup():
        import jax, jax.numpy as jnp
        import numpy as np
        D_MODEL = 128
        N_HEADS = 16
        key = jax.random.key(seed)
        k1, k2, k3, k4 = jax.random.split(key, 4)
        B, T, D = (4, 256, D_MODEL)
        x = jax.random.normal(k1, (B, T, D), dtype=jnp.float32)
        w_qkv = jax.random.normal(k2, (D, 3 * D), dtype=jnp.float32) / np.sqrt(D)
        w_out = jax.random.normal(k3, (D, D), dtype=jnp.float32) / np.sqrt(D)
        b_out = jax.random.normal(k4, (D,), dtype=jnp.float32) * 0.01
        return {'x': x, 'w_qkv': w_qkv, 'w_out': w_out, 'b_out': b_out}
    _L0_attn_in = _L0_attn_setup()

    def _L0_ffn_setup():
        import jax, jax.numpy as jnp
        import numpy as np
        B, S, D, H, L, E, K = (4, 128, 128, 16, 2, 8, 2)
        DFF = 4 * D

        def _ln(x, w, b):
            m = x.mean(-1, keepdims=True)
            v = x.var(-1, keepdims=True)
            return (x - m) / jnp.sqrt(v + 1e-05) * w + b

        def _attn(x, wq, wk, wv, wo, bq, bk, bv, bo):
            Bb, T, C = x.shape
            hd = C // H
            q = (x @ wq + bq).reshape(Bb, T, H, hd).transpose(0, 2, 1, 3)
            k = (x @ wk + bk).reshape(Bb, T, H, hd).transpose(0, 2, 1, 3)
            v = (x @ wv + bv).reshape(Bb, T, H, hd).transpose(0, 2, 1, 3)
            att = jnp.einsum('bhqd,bhkd->bhqk', q, k) * hd ** (-0.5)
            causal = jnp.tril(jnp.ones((T, T), bool))
            att = jnp.where(causal, att, -jnp.inf)
            att = jax.nn.softmax(att, axis=-1)
            y = jnp.einsum('bhqk,bhkd->bhqd', att, v).transpose(0, 2, 1, 3).reshape(Bb, T, C)
            return y @ wo + bo

        def _ffn(h, w1, b1, w2, b2):
            return jax.nn.gelu(h @ w1 + b1, approximate=False) @ w2 + b2

        def _combine_weights(logits):
            vals, idx = jax.lax.top_k(logits, K)
            w = jax.nn.softmax(vals, axis=-1)
            onehot = (idx[..., None] == jnp.arange(E)).astype(w.dtype)
            return jnp.sum(w[..., None] * onehot, axis=-2)

        def _token_moe(h, gw, gb, w1, b1, w2, b2):
            cw = _combine_weights(h @ gw + gb)
            out = jnp.zeros_like(h)
            for e in range(E):
                out = out + _ffn(h, w1[e], b1[e], w2[e], b2[e]) * cw[..., e:e + 1]
            return out

        def _seq_moe(h, gw, gb, w1, b1, w2, b2):
            cw = _combine_weights(h.mean(axis=1) @ gw + gb)
            out = jnp.zeros_like(h)
            for e in range(E):
                out = out + _ffn(h, w1[e], b1[e], w2[e], b2[e]) * cw[:, e, None, None]
            return out
        key = jax.random.key(seed)
        ks = jax.random.split(key, 9)
        n = lambda k, shp: jax.random.normal(k, shp, dtype=jnp.float32) * 0.02
        return {'x': jax.random.normal(ks[0], (B, S, D), dtype=jnp.float32), 'ln1_w': jnp.ones((L, D), jnp.float32), 'ln1_b': jnp.zeros((L, D), jnp.float32), 'ln2_w': jnp.ones((L, D), jnp.float32), 'ln2_b': jnp.zeros((L, D), jnp.float32), 'wq': n(ks[1], (L, D, D)), 'wk': n(ks[2], (L, D, D)), 'wv': n(ks[3], (L, D, D)), 'wo': n(ks[4], (L, D, D)), 'bq': jnp.zeros((L, D), jnp.float32), 'bk': jnp.zeros((L, D), jnp.float32), 'bv': jnp.zeros((L, D), jnp.float32), 'bo': jnp.zeros((L, D), jnp.float32), 'gate_w': n(ks[5], (L, D, E)), 'gate_b': jnp.zeros((L, E), jnp.float32), 'e_w1': n(ks[6], (L, E, D, DFF)), 'e_b1': jnp.zeros((L, E, DFF), jnp.float32), 'e_w2': n(ks[7], (L, E, DFF, D)), 'e_b2': jnp.zeros((L, E, D), jnp.float32)}
    _L0_ffn_in = _L0_ffn_setup()
    _d = {'L0_attn_x': _L0_attn_in['x'], 'L0_attn_w_qkv': _L0_attn_in['w_qkv'], 'L0_attn_w_out': _L0_attn_in['w_out'], 'L0_attn_b_out': _L0_attn_in['b_out'], 'L0_ffn_ln1_w': _L0_ffn_in['ln1_w'], 'L0_ffn_ln1_b': _L0_ffn_in['ln1_b'], 'L0_ffn_ln2_w': _L0_ffn_in['ln2_w'], 'L0_ffn_ln2_b': _L0_ffn_in['ln2_b'], 'L0_ffn_wq': _L0_ffn_in['wq'], 'L0_ffn_wk': _L0_ffn_in['wk'], 'L0_ffn_wv': _L0_ffn_in['wv'], 'L0_ffn_wo': _L0_ffn_in['wo'], 'L0_ffn_bq': _L0_ffn_in['bq'], 'L0_ffn_bk': _L0_ffn_in['bk'], 'L0_ffn_bv': _L0_ffn_in['bv'], 'L0_ffn_bo': _L0_ffn_in['bo'], 'L0_ffn_gate_w': _L0_ffn_in['gate_w'], 'L0_ffn_gate_b': _L0_ffn_in['gate_b'], 'L0_ffn_e_w1': _L0_ffn_in['e_w1'], 'L0_ffn_e_b1': _L0_ffn_in['e_b1'], 'L0_ffn_e_w2': _L0_ffn_in['e_w2'], 'L0_ffn_e_b2': _L0_ffn_in['e_b2']}
    _x0 = _d['L0_attn_x']
    _d['L0_attn_x'] = jax.random.normal(jax.random.fold_in(jax.random.key(seed), 1), (16, 256, 128), dtype=_x0.dtype)
    del _x0
    return _d

def reference(L0_attn_x, L0_attn_w_qkv, L0_attn_w_out, L0_attn_b_out, L0_ffn_ln1_w, L0_ffn_ln1_b, L0_ffn_ln2_w, L0_ffn_ln2_b, L0_ffn_wq, L0_ffn_wk, L0_ffn_wv, L0_ffn_wo, L0_ffn_bq, L0_ffn_bk, L0_ffn_bv, L0_ffn_bo, L0_ffn_gate_w, L0_ffn_gate_b, L0_ffn_e_w1, L0_ffn_e_b1, L0_ffn_e_w2, L0_ffn_e_b2):

    def _L0_attn_ref(x, w_qkv, w_out, b_out):
        import jax, jax.numpy as jnp
        import numpy as np
        D_MODEL = 128
        N_HEADS = 16
        B, T, D = x.shape
        h = N_HEADS
        Hd = D // h
        qkv = jnp.einsum('btd,de->bte', x, w_qkv).reshape(B, T, 3, h, Hd)
        q = jnp.transpose(qkv[:, :, 0], (0, 2, 1, 3))
        k = jnp.transpose(qkv[:, :, 1], (0, 2, 1, 3))
        v = jnp.transpose(qkv[:, :, 2], (0, 2, 1, 3))
        scale = 1.0 / jnp.sqrt(jnp.array(Hd, dtype=x.dtype))
        logits = jnp.einsum('bhqd,bhkd->bhqk', q, k) * scale
        mask = jnp.tril(jnp.ones((T, T), dtype=x.dtype))
        big_neg = jnp.array(-10000000000.0, dtype=x.dtype)
        logits = logits + (1.0 - mask)[None, None, :, :] * big_neg
        attn = jax.nn.softmax(logits, axis=-1)
        out = jnp.einsum('bhqk,bhkd->bhqd', attn, v)
        out = jnp.transpose(out, (0, 2, 1, 3)).reshape(B, T, D)
        return jnp.einsum('btd,de->bte', out, w_out) + b_out

    def _L0_ffn_ref(x, ln1_w, ln1_b, ln2_w, ln2_b, wq, wk, wv, wo, bq, bk, bv, bo, gate_w, gate_b, e_w1, e_b1, e_w2, e_b2):
        import jax, jax.numpy as jnp
        import numpy as np
        B, S, D, H, L, E, K = (4, 128, 128, 16, 2, 8, 2)
        DFF = 4 * D

        def _ln(x, w, b):
            m = x.mean(-1, keepdims=True)
            v = x.var(-1, keepdims=True)
            return (x - m) / jnp.sqrt(v + 1e-05) * w + b

        def _attn(x, wq, wk, wv, wo, bq, bk, bv, bo):
            Bb, T, C = x.shape
            hd = C // H
            q = (x @ wq + bq).reshape(Bb, T, H, hd).transpose(0, 2, 1, 3)
            k = (x @ wk + bk).reshape(Bb, T, H, hd).transpose(0, 2, 1, 3)
            v = (x @ wv + bv).reshape(Bb, T, H, hd).transpose(0, 2, 1, 3)
            att = jnp.einsum('bhqd,bhkd->bhqk', q, k) * hd ** (-0.5)
            causal = jnp.tril(jnp.ones((T, T), bool))
            att = jnp.where(causal, att, -jnp.inf)
            att = jax.nn.softmax(att, axis=-1)
            y = jnp.einsum('bhqk,bhkd->bhqd', att, v).transpose(0, 2, 1, 3).reshape(Bb, T, C)
            return y @ wo + bo

        def _ffn(h, w1, b1, w2, b2):
            return jax.nn.gelu(h @ w1 + b1, approximate=False) @ w2 + b2

        def _combine_weights(logits):
            vals, idx = jax.lax.top_k(logits, K)
            w = jax.nn.softmax(vals, axis=-1)
            onehot = (idx[..., None] == jnp.arange(E)).astype(w.dtype)
            return jnp.sum(w[..., None] * onehot, axis=-2)

        def _token_moe(h, gw, gb, w1, b1, w2, b2):
            cw = _combine_weights(h @ gw + gb)
            out = jnp.zeros_like(h)
            for e in range(E):
                out = out + _ffn(h, w1[e], b1[e], w2[e], b2[e]) * cw[..., e:e + 1]
            return out

        def _seq_moe(h, gw, gb, w1, b1, w2, b2):
            cw = _combine_weights(h.mean(axis=1) @ gw + gb)
            out = jnp.zeros_like(h)
            for e in range(E):
                out = out + _ffn(h, w1[e], b1[e], w2[e], b2[e]) * cw[:, e, None, None]
            return out
        for l in range(L):
            x = x + _attn(_ln(x, ln1_w[l], ln1_b[l]), wq[l], wk[l], wv[l], wo[l], bq[l], bk[l], bv[l], bo[l])
            h = _ln(x, ln2_w[l], ln2_b[l])
            moe = _token_moe if l % 2 == 0 else _seq_moe
            x = x + moe(h, gate_w[l], gate_b[l], e_w1[l], e_b1[l], e_w2[l], e_b2[l])
        return x
    x = L0_attn_x
    x = x + _layernorm(_L0_attn_ref(_layernorm(x, axis=-1), L0_attn_w_qkv, L0_attn_w_out, L0_attn_b_out), axis=-1)
    x = x + _layernorm(_L0_ffn_ref(_layernorm(x, axis=-1), L0_ffn_ln1_w, L0_ffn_ln1_b, L0_ffn_ln2_w, L0_ffn_ln2_b, L0_ffn_wq, L0_ffn_wk, L0_ffn_wv, L0_ffn_wo, L0_ffn_bq, L0_ffn_bk, L0_ffn_bv, L0_ffn_bo, L0_ffn_gate_w, L0_ffn_gate_b, L0_ffn_e_w1, L0_ffn_e_b1, L0_ffn_e_w2, L0_ffn_e_b2), axis=-1)
    return x

_drawn_inputs = setup_inputs


def setup_inputs(seed=0):
    import zlib

    import numpy as np

    out = dict(_drawn_inputs(seed))
    spreads = {'L0_ffn_ln1_w': (1.0, 0.6),
     'L0_ffn_ln1_b': (0.0, 0.8),
     'L0_ffn_ln2_w': (1.0, 0.6),
     'L0_ffn_ln2_b': (0.0, 0.745),
     'L0_ffn_bq': (0.0, 0.8),
     'L0_ffn_bk': (0.0, 0.8),
     'L0_ffn_bv': (0.0, 0.552),
     'L0_ffn_bo': (0.0, 0.1),
     'L0_ffn_gate_b': (0.0, 0.1),
     'L0_ffn_e_b1': (0.0, 0.8),
     'L0_ffn_e_b2': (0.0, 0.1)}
    factors = {'L0_ffn_wq': 8.0, 'L0_ffn_wk': 8.0, 'L0_ffn_wv': 4.259, 'L0_ffn_wo': 2.996}
    for name, (base, spread) in spreads.items():
        noise = np.random.default_rng([zlib.crc32(name.encode()), seed]).standard_normal(out[name].shape)
        drawn = base * np.exp(spread * noise) if base else spread * noise
        out[name] = jnp.asarray(drawn.astype(out[name].dtype))
    for name, factor in factors.items():
        out[name] = (out[name] * factor).astype(out[name].dtype)
    return out
```

```python
from contextlib import ExitStack

import numpy as np

import concourse.bass as bass
from concourse import mybir

ALU = mybir.AluOpType
ACT = mybir.ActivationFunctionType
AX = mybir.AxisListType
F32 = mybir.dt.float32
BF16 = mybir.dt.bfloat16
I32 = mybir.dt.int32

P = 128
H = 16
HD = P // H
HG = 4
NG = H // HG
E = 8
TOP = 2
EPS = 1e-5
SCALE = float(HD) ** -0.5
MASKED = -1e30
TERM = [(0, 0), (0, 1), (0, 2), (1, 0), (1, 1), (2, 0)]
TERMS = len(TERM)
ROWS = TERMS * HD
SHIFT = ROWS + 2
NPRE, NRSTD, NRES, NSPLIT = 4, 4, 14, 4
STACK_DMAS = 12


def need(eng, sem, value):
    if isinstance(value, int) and value <= 0:
        return
    eng.wait_ge(sem, value)


def build(nc, x_in, w_qk, w_v, w_o, b_qk, b_v, b_o, ln1, ln2, gate_w, gate_b, e_w1, e_b1, e_w2, e_b2, out):
    B, T, D = x_in.shape
    assert D == P and T == 2 * P and B % 2 == 0 and B >= 8
    L, _, _, DFF = e_w1.shape
    FC = DFF // P
    NT = B * 2

    pe, act, dve, pool, sp = nc.tensor, nc.scalar, nc.vector, nc.gpsimd, nc.sync

    with ExitStack() as ctx:
        def sb(name, shape, dt=F32):
            return ctx.enter_context(nc.sbuf_tensor(name, shape, dt))

        def sem(name):
            return ctx.enter_context(nc.semaphore(name))

        bank = [ctx.enter_context(nc.psum_tensor(f"bank{i}", [P, 512], F32)) for i in range(8)]
        max_bank, exp_bank = bank[0:2], bank[2:4]
        pv_bank, pre_bank, mid_bank, post_bank = bank[4:8]

        x_all = sb("x_all", [P, NT, P])
        f_all = sb("f_all", [P, NT, P])
        hT_all = sb("hT_all", [P, NT * P])
        wqk_s = sb("wqk_s", [P, 3, 2, P])
        wv_s = sb("wv_s", [P, 3, P])
        wo_s = sb("wo_s", [P, 3, P])
        bqk_s = sb("bqk_s", [P, 3, 2])
        bv_s = sb("bv_s", [P, 3, P])
        bo_s = sb("bo_s", [P, 3, P])
        ln1_s = sb("ln1_s", [P, 3, 2])
        ln2_s = sb("ln2_s", [P, L, 2])
        gw_s = sb("gw_s", [P, L, E])
        gb_s = sb("gb_s", [P, L, E])
        w1_s = sb("w1_s", [P, E, DFF])
        w2_s = sb("w2_s", [P, E, FC, P])
        b1_s = sb("b1_s", [P, L, E, FC])
        b2_s = sb("b2_s", [E, L, P])
        ident = sb("ident", [P, P])
        identb = sb("identb", [P, P], BF16)
        maskneg = sb("maskneg", [P, HG, P], BF16)
        ones = sb("ones", [P, P])
        power = sb("power", [P, 2])
        iota_e = sb("iota_e", [P, E])
        pre_st = sb("pre_st", [P, 2, 6])
        pre_mv = sb("pre_mv", [P, 2, 2, 2])
        pre_r = sb("pre_r", [P, 2, 2])
        xn = sb("xn", [P, 2, 2, P])
        xT = sb("xT", [P, 2, T])
        qkf = sb("qkf", [P, 2, T])
        rest = sb("rest", [P, 2, T])
        parts = sb("parts", [P, 2, 3, 2, T], BF16)
        qstack = sb("qstack", [SHIFT, 2, H, T], BF16)
        kstack = sb("kstack", [SHIFT, 2, H, T], BF16)
        vaug = sb("vaug", [P, 2, 2, H, 32])
        negm = sb("negm", [P, 2, 2, HG])
        mparts = sb("mparts", [P, 2, 2, 2, HG], BF16)
        mT = sb("mT", [2 * HG, 2, T], BF16)
        prob1 = sb("prob1", [P, 2, HG, P])
        prob0 = sb("prob0", [P, 2, HG, T])
        oT = sb("oT", [P, 2, NG, T])
        rden = sb("rden", [P, 2, H])
        on = sb("on", [P, 2, 2, P])
        onT = sb("onT", [P, 2, T])
        att = sb("att", [P, 2, 2, P])
        post_st = sb("post_st", [P, 2, 6])
        post_mv = sb("post_mv", [P, 2, 2, 2])
        post_r = sb("post_r", [P, 2, 2])
        st2 = sb("st2", [P, 2, 6])
        mv2 = sb("mv2", [P, 2, 2, 2])
        r2 = sb("r2", [P, 2, 2])
        hn = sb("hn", [P, 2, 2, P])
        hT = sb("hT", [P, 2, T])
        logits = sb("logits", [P, NT, E])
        hmean = sb("hmean", [P, B])
        gtmp = sb("gtmp", [P, 5, NT, E])
        gsm = sb("gsm", [P, 7, NT])
        cw = sb("cw", [P, NT, E])
        hid = prob0
        cwt = sb("cwt", [P, 2, E])
        cwT = sb("cwT", [E, T])
        chosen = sb("chosen", [P, TOP, B], I32)
        w1_job = sb("w1_job", [P, TOP, DFF])
        w2_job = sb("w2_job", [P, TOP, FC, P])
        b1_job = sb("b1_job", [P, TOP, FC])

        const_ok, waited = sem("const_ok"), sem("waited")
        vconst_ok = sem("vconst_ok")
        x_first, x_rest = sem("x_first"), sem("x_rest")
        small_ld = sem("small_ld")
        expert_ld = [sem("expert_ld0"), sem("expert_ld1")]
        pre_stats, pre_rstd, xn_ok = sem("pre_stats"), sem("pre_rstd"), sem("xn_ok")
        xT_ps, xT_sb, qk_ps, v_ps = sem("xT_ps"), sem("xT_sb"), sem("qk_ps"), sem("v_ps")
        qkf_sb, split, v_sb = sem("qkf_sb"), sem("split"), sem("v_sb")
        stack_dma = [sem("stack_dma0"), sem("stack_dma1")]
        row_dma = [sem("row_dma0"), sem("row_dma1")]
        max_ps, max_done, negmax = sem("max_ps"), sem("max_done"), sem("negmax")
        maxT_ps, mT_sb = sem("maxT_ps"), sem("mT_sb")
        sT_ps, exp_done, sel_done, pv_ps, ot_sb = sem("sT_ps"), sem("exp_done"), sem("sel_done"), sem("pv_ps"), sem("ot_sb")
        o1_ps, attn_n, o2_ps, onT_sb, o3_ps = sem("o1_ps"), sem("attn_n"), sem("o2_ps"), sem("onT_sb"), sem("o3_ps")
        res, post_rstd = sem("res"), sem("post_rstd")
        hT_ps, hT_sb, hT_kept, lg_ps, lg_sb = sem("hT_ps"), sem("hT_sb"), sem("hT_kept"), sem("lg_ps"), sem("lg_sb")
        gate_v, gate_a, gate_p = sem("gate_v"), sem("gate_a"), sem("gate_p")
        h_ps, gelu_done, y_ps, acc = sem("h_ps"), sem("gelu_done"), sem("y_ps"), sem("acc")
        w1_got, w2_got = sem("w1_got"), sem("w2_got")
        cw_copied, cwT_ps, cwT_sb, b2_ps, b2_add = sem("cw_copied"), sem("cwT_ps"), sem("cwT_sb"), sem("b2_ps"), sem("b2_add")
        fin_v, fin_p, fin_n, fin_x, out_dma = sem("fin_v"), sem("fin_p"), sem("fin_n"), sem("fin_x"), sem("out_dma")

        SMALL = 12 * 16
        x_dram = x_in.rearrange("b (j p) d -> p (b j) d", p=P)
        out_dram = out.rearrange("b (j p) d -> p (b j) d", p=P)

        class Item:
            def __init__(self, v, par, phase):
                self.v, self.par, self.phase = v, par, phase
                self.b = v - phase * B

        def item(step, d):
            n, par, phase, lo, hi = step
            if isinstance(n, int):
                v = n + d
                return Item(v, v % 2, v // B) if lo <= v < hi else None
            return Item(n + d, (par + d) % 2, phase)

        def group(step, k, lag):
            d, g = divmod(k - lag, NG)
            return item(step, d), g

        def run_steps(eng, slot, lo, hi):
            def peeled(a, b):
                for n in range(a, b):
                    for k in range(NG):
                        slot((n, n % 2, None, lo, hi), k)

            at = lo - 2
            for phase in range(lo // B, hi // B):
                first, last = phase * B + 4, phase * B + B - 2
                peeled(at, first)
                with eng.Fori(first, last - 1, 2) as n:
                    for d in range(2):
                        for k in range(NG):
                            slot((n + d, d, phase, lo, hi), k)
                at = last
            peeled(at, hi + 3)

        def alone(eng):
            eng.sem_inc(waited, 1)

        def unit(i, g, u):
            return 12 * i.v + 3 * g + u + 1

        def stack_ready(i):
            return 8 * STACK_DMAS * (i.v + (2 if i.par == 0 else 1))

        def rows_ready(i, g):
            return 32 * i.v + 16 * (g // 2 + 1)

        def pe_max(i, g, u):
            p0 = HG * g
            if g == 0 and u == 0:
                pe.wait_ge(stack_dma[i.par], stack_ready(i))
            need(pe, max_done, unit(i, g, u) - 2)
            bk = max_bank[(g + u) % 2]
            q, k = qstack[0:ROWS, i.par], kstack[0:ROWS, i.par]
            if u == 0:
                o = bk[:].rearrange("p (h k) -> p h k", h=HG)
                nc.tensor.matmul(o, identb[:], maskneg[:], start=True, stop=False, skip_group_check=True)
                for h in range(HG):
                    m = nc.tensor.matmul(o[:, h], q[:, p0 + h, 0:P], k[:, p0 + h, 0:P],
                                         start=False, stop=True, skip_group_check=True)
            else:
                o = bk[:].rearrange("p (h k) -> p h k", h=2)
                nc.tensor.matmul(o[:, :, P:T], identb[:], maskneg[:, 0:2], start=True, stop=False,
                                 skip_group_check=True)
                for h in range(2):
                    hh = p0 + 2 * (u - 1) + h
                    m = nc.tensor.matmul(o[:, h], q[:, hh, P:T], k[:, hh, :],
                                         start=False, stop=True, skip_group_check=True)
            m.then_inc(max_ps, 1)

        def pe_scores(i, g, u):
            p0 = HG * g
            if u == 0:
                pe.wait_ge(row_dma[g % 2], rows_ready(i, g))
            need(pe, exp_done, unit(i, g, u) - 2)
            bk = exp_bank[(g + u) % 2]
            q, k = qstack[:, i.par], kstack[:, i.par]
            if u == 0:
                for h in range(HG):
                    m = nc.tensor.matmul(bk[:, h * P:(h + 1) * P], k[:, p0 + h, P:T], q[:, p0 + h, P:T],
                                         start=True, stop=True)
            else:
                for h in range(2):
                    hh = p0 + 2 * (u - 1) + h
                    m = nc.tensor.matmul(bk[:, h * T:(h + 1) * T], k[:, hh, 0:P], q[:, hh, :],
                                         start=True, stop=True)
            m.then_inc(sT_ps, 1)

        def pe_values(i, g, half):
            G = 4 * i.v + g
            if half == 0:
                need(pe, v_sb, i.v + 1)
                pe.wait_ge(sel_done, 2 * G + 2)
                need(pe, ot_sb, G)
            for h in range(2 * half, 2 * half + 2):
                head = HG * g + h
                o = pv_bank[32 * h:32 * h + 32, 0:T]
                nc.tensor.matmul(o, vaug[:, i.par, 0, head], prob0[:, g % 2, h], start=True, stop=False,
                                 skip_group_check=True)
                m = nc.tensor.matmul(o[:, P:T], vaug[:, i.par, 1, head], prob1[:, g % 2, h],
                                     start=False, stop=True, skip_group_check=True)
            if half == 1:
                m.then_inc(pv_ps, 1)

        def pe_max_T(i, g):
            G = 4 * i.v + g
            pe.wait_ge(negmax, 2 * G + 2)
            need(pe, mT_sb, G)
            o = mid_bank[0:2 * HG, 0:P].bitcast(BF16)
            for qb in range(2):
                m = nc.tensor.transpose(o[:, qb * P:(qb + 1) * P],
                                        mparts[:, g % 2, qb].rearrange("p a h -> p (a h)"), identb[:])
            m.then_inc(maxT_ps, 1)

        def pe_xT(i):
            pe.wait_ge(xn_ok, 2 * i.v + 2)
            need(pe, qkf_sb, 2 * i.v)
            for j in range(2):
                m = nc.tensor.transpose(pre_bank[:, j * P:(j + 1) * P], xn[:, i.par, j], ident[:])
            m.then_inc(xT_ps, 1)

        def pe_qk(i):
            pe.wait_ge(xT_sb, i.v + 1)
            for t in range(2):
                m = nc.tensor.matmul(pre_bank[:, t * T:(t + 1) * T], wqk_s[:, i.phase, t], xT[:, i.par],
                                     start=True, stop=True)
            m.then_inc(qk_ps, 1)

        def pe_v(i):
            need(pe, mT_sb, 4 * i.v - 2)
            for j in range(2):
                m = nc.tensor.matmul(mid_bank[:, j * P:(j + 1) * P], xT[:, i.par, j * P:(j + 1) * P],
                                     wv_s[:, i.phase], start=True, stop=True)
            m.then_inc(v_ps, 1)

        def pe_o1(i, qb):
            if qb == 0:
                pe.wait_ge(ot_sb, 4 * i.v + 4)
                need(pe, res, NRES * (i.v - 1) + 1)
                before = Item(i.v - 1, 1 - i.par, (i.v - 1) // B if isinstance(i.v, int) else i.phase)
                if before.phase > 0:
                    need(pe, hT_sb, before.v - B + 1)
            else:
                pe.wait_ge(attn_n, 4 * i.v + 2)
            for g in range(NG):
                m = nc.tensor.transpose(post_bank[:, g * P:(g + 1) * P], oT[:, i.par, g, qb * P:(qb + 1) * P],
                                        ident[:])
            m.then_inc(o1_ps, 1)

        def pe_o2(i):
            pe.wait_ge(attn_n, 4 * i.v + 4)
            for qb in range(2):
                m = nc.tensor.transpose(post_bank[:, qb * P:(qb + 1) * P], on[:, i.par, qb], ident[:])
            m.then_inc(o2_ps, 1)

        def pe_o3(i):
            pe.wait_ge(onT_sb, i.v + 1)
            for qb in range(2):
                m = nc.tensor.matmul(post_bank[:, qb * P:(qb + 1) * P], onT[:, i.par, qb * P:(qb + 1) * P],
                                     wo_s[:, i.phase], start=True, stop=True)
            m.then_inc(o3_ps, 1)

        def pe_hT(i):
            pe.wait_ge(res, NRES * i.v + NRES)
            for j in range(2):
                m = nc.tensor.transpose(post_bank[:, j * P:(j + 1) * P], hn[:, i.par, j], ident[:])
            m.then_inc(hT_ps, 1)

        def pe_logits(i):
            pe.wait_ge(hT_sb, i.v - B + 1)
            at = 4 * i.v + 11
            pe.wait_ge(mT_sb, min(at, 8 * B) if isinstance(at, int) else at)
            for j in range(2):
                m = nc.tensor.matmul(mid_bank[:, j * E:(j + 1) * E], hT[:, i.par, j * P:(j + 1) * P],
                                     gw_s[:, 0], start=True, stop=True)
            m.then_inc(lg_ps, 1)

        def pe_slot(step, k):
            cur, nxt, old, older = (item(step, d) for d in (0, 1, -1, -2))
            (ie, ge), (iv, gv), (im, gm) = group(step, k, 2), group(step, k, 3), group(step, k, 1)
            if cur:
                pe_max(cur, k, 0)
            if ie:
                pe_scores(ie, ge, 0)
            if im:
                if k == 3 and nxt:
                    pe.wait_ge(v_sb, nxt.v + 1)
                if k == 0 and im.phase == 1:
                    need(pe, lg_sb, im.v - B - 1)
                pe_max_T(im, gm)
            if k == 0 and older:
                pe_o2(older)
            if k == 0 and nxt:
                pe_xT(nxt)
            if k == 3 and old:
                pe_o1(old, 0)
            if cur:
                pe_max(cur, k, 1)
            if ie:
                pe_scores(ie, ge, 1)
            if iv:
                pe_values(iv, gv, 0)
            if k == 2 and older and older.phase > 0:
                pe_hT(older)
            if cur:
                pe_max(cur, k, 2)
            if ie:
                pe_scores(ie, ge, 2)
            if iv:
                pe_values(iv, gv, 1)
            if k == 0 and older:
                pe_o3(older)
            if k == 1 and nxt:
                pe_qk(nxt)
            if k == 2 and nxt:
                pe_v(nxt)
            if k == 3 and older and older.phase == 1:
                pe_logits(older)
            if k == 3 and old:
                pe_o1(old, 1)

        def act_exp(i, g, u):
            act.wait_ge(sT_ps, unit(i, g, u))
            if u == 0:
                need(act, pv_ps, 4 * i.v + g - 1)
            bk = exp_bank[(g + u) % 2]
            if u == 0:
                o, s = prob1[:, g % 2].rearrange("p h q -> p (h q)"), bk[:]
            else:
                o, s = prob0[:, g % 2, 2 * u - 2:2 * u].rearrange("p h q -> p (h q)"), bk[:]
            nc.scalar.activation(o, s, ACT.Exp, scale=SCALE).then_inc(exp_done, 1)

        def act_oT(i, g):
            act.wait_ge(pv_ps, 4 * i.v + g + 1)
            if g == 0:
                need(act, o1_ps, 2 * (i.v - 2) + 2)
            nc.scalar.copy(oT[:, i.par, g], pv_bank[:, 0:T]).then_inc(ot_sb, 1)

        def act_stack(i, terms):
            if terms[0] == 0:
                act.wait_ge(split, NSPLIT * i.v + NSPLIT)
                need(act, sT_ps, 12 * (i.v - 2) + 12)
            for t in terms:
                for which, stack in enumerate((qstack, kstack)):
                    act.dma_start(stack[t * HD:(t + 1) * HD, i.par], parts[:, i.par, TERM[t][which], which])\
                       .then_inc(stack_dma[i.par], 16)

        def act_slot(step, k):
            cur, nxt, old, older = (item(step, d) for d in (0, 1, -1, -2))
            (ie, ge), (io, go) = group(step, k, 2), group(step, k, 4)
            if io:
                act_oT(io, go)
            if k == 2 and nxt:
                act.wait_ge(qk_ps, nxt.v + 1)
                need(act, split, NSPLIT * (nxt.v - 1) + 2)
                for t in range(2):
                    nc.scalar.activation(qkf[:, t], pre_bank[:, t * T:(t + 1) * T], ACT.Identity,
                                         bias=bqk_s[:, nxt.phase, t:t + 1]).then_inc(qkf_sb, 1)
            if ie:
                act_exp(ie, ge, 0)
            if k == 0 and older:
                act.wait_ge(o2_ps, older.v + 1)
                need(act, o3_ps, older.v - 1)
                nc.scalar.copy(onT[:, older.par], post_bank[:, 0:T]).then_inc(onT_sb, 1)
            if k == 0 and nxt:
                act.wait_ge(xT_ps, nxt.v + 1)
                need(act, v_ps, nxt.v - 1)
                nc.scalar.activation(xT[:, nxt.par], pre_bank[:, 0:T], ACT.Identity,
                                     scale=ln1_s[:, nxt.phase, 0:1], bias=ln1_s[:, nxt.phase, 1:2])\
                  .then_inc(xT_sb, 1)
            if ie:
                act_exp(ie, ge, 1)
            if ie:
                act_exp(ie, ge, 2)
            if k == 2 and nxt:
                act_stack(nxt, (0, 1, 2))
            if k == 3 and nxt:
                act_stack(nxt, (3, 4, 5))
            if k == 2 and older and older.phase > 0:
                act.wait_ge(hT_ps, older.v - B + 1)
                need(act, hT_kept, older.v - B - 1)
                if older.phase == 1:
                    need(act, lg_ps, older.v - B - 1)
                else:
                    need(act, lg_sb, older.v - B - 1)
                nc.scalar.activation(hT[:, older.par], post_bank[:, 0:T], ACT.Identity,
                                     scale=ln2_s[:, older.phase - 1, 0:1], bias=ln2_s[:, older.phase - 1, 1:2])\
                  .then_inc(hT_sb, 1)

        def dve_reduce(i, g, u):
            dve.wait_ge(max_ps, unit(i, g, u))
            if u == 0:
                need(dve, negmax, 2 * (4 * i.v + g) - 2)
            bk = max_bank[(g + u) % 2]
            if u == 0:
                o, s = negm[:, g % 2, 0], bk[:].rearrange("p (h k) -> p h k", h=HG)
            else:
                o, s = negm[:, g % 2, 1, 2 * u - 2:2 * u], bk[:].rearrange("p (h k) -> p h k", h=2)
            nc.vector.tensor_reduce(o, s, AX.X, ALU.max, negate=True).then_inc(max_done, 1)

        def dve_split_max(i, g):
            G = 4 * i.v + g
            dve.wait_ge(max_done, unit(i, g, 2))
            need(dve, maxT_ps, G - 1)
            nc.vector.tensor_copy(mparts[:, g % 2, :, 0], negm[:, g % 2]).then_inc(negmax, 1)
            dve.wait_ge(negmax, 2 * G + 1)
            nc.vector.tensor_tensor(mparts[:, g % 2, :, 1], negm[:, g % 2], mparts[:, g % 2, :, 0],
                                    ALU.subtract).then_inc(negmax, 1)

        def dve_mT(i, g):
            dve.wait_ge(maxT_ps, 4 * i.v + g + 1)
            need(dve, row_dma[g % 2], rows_ready(i, g) - 16)
            nc.vector.tensor_copy(mT[:, g % 2], mid_bank[0:2 * HG, 0:P].bitcast(BF16)).then_inc(mT_sb, 1)

        def dve_split(i):
            base = NSPLIT * i.v
            dve.wait_ge(qkf_sb, 2 * i.v + 2)
            need(dve, stack_dma[i.par], stack_ready(i) - 16 * STACK_DMAS)
            pt = parts[:, i.par]
            nc.vector.tensor_copy(pt[:, 0], qkf[:]).then_inc(split, 1)
            dve.wait_ge(split, base + 1)
            nc.vector.tensor_tensor(rest[:], qkf[:], pt[:, 0], ALU.subtract).then_inc(split, 1)
            dve.wait_ge(split, base + 2)
            nc.vector.tensor_copy(pt[:, 1], rest[:]).then_inc(split, 1)
            dve.wait_ge(split, base + 3)
            nc.vector.tensor_tensor(pt[:, 2], rest[:], pt[:, 1], ALU.subtract).then_inc(split, 1)

        def dve_norm(i, qb):
            dve.wait_ge(o1_ps, 2 * i.v + qb + 1)
            o = post_bank[:].rearrange("p (h c) -> p h c", c=32)
            need(dve, o2_ps, i.v - 1)
            nc.vector.reciprocal(rden[:, qb], o[:, :, HD]).then_inc(attn_n, 1)
            dve.wait_ge(attn_n, 4 * i.v + 2 * qb + 1)
            nc.vector.tensor_tensor(on[:, i.par, qb].rearrange("p (h d) -> p h d", d=HD), o[:, :, 0:HD],
                                    rden[:, qb].unsqueeze(2).to_broadcast([P, H, HD]),
                                    ALU.mult).then_inc(attn_n, 1)

        def dve_stats(src, st, mv, s, base):
            need(dve, s, base)
            alone(dve)
            for j in range(2):
                nc.vector.bn_stats(st[:, j], src[j]).then_inc(s, 1)
            dve.wait_ge(s, base + 2)
            alone(dve)
            for j in range(2):
                nc.vector.bn_aggr(mv[:, j], st[:, j]).then_inc(s, 1)

        def tiles(t, i):
            return [t[:, bass.ds(2 * i.b + j, 1), :].rearrange("p a d -> p (a d)") for j in range(2)]

        def pair(t, i):
            return t[:, bass.ds(2 * i.b, 2), :]

        def dve_normal(dst, src, mv, r, s, last=1):
            for j in range(2):
                nc.vector.tensor_scalar(dst[j], src[j], mv[:, j, 0:1], r[:, j:j + 1],
                                        ALU.subtract, ALU.mult).then_inc(s, last if j else 1)

        def dve_residual(i):
            base = NRES * i.v
            dve.wait_ge(o3_ps, i.v + 1)
            nc.vector.tensor_tensor(att[:, i.par], post_bank[:, 0:T].rearrange("p (j d) -> p j d", j=2),
                                    bo_s[:, i.phase:i.phase + 1].to_broadcast([P, 2, P]),
                                    ALU.add).then_inc(res, 1)
            dve.wait_ge(res, base + 1)
            if i.phase > 0:
                nc.vector.tensor_tensor(pair(f_all, i), pair(f_all, i), att[:, i.par], ALU.add).then_inc(res, 1)
            src = tiles(f_all, i) if i.phase > 0 else [att[:, i.par, j] for j in range(2)]
            need(dve, post_rstd, NRSTD * (i.v - 2) + 2)
            dve_stats(src, post_st, post_mv[:, i.par], res, base + (2 if i.phase > 0 else 1))

        def dve_after(i):
            base = NRES * i.v
            dve.wait_ge(post_rstd, NRSTD * i.v + (2 if i.phase == 0 else NRSTD))
            if i.phase > 0:
                need(dve, hT_ps, i.v - B - 1)
                dve_normal([hn[:, i.par, j] for j in range(2)], tiles(f_all, i), post_mv[:, i.par],
                           post_r[:, i.par], res, NRES - 7)
                return
            att_j = [att[:, i.par, j] for j in range(2)]
            dve_normal(att_j, att_j, post_mv[:, i.par], post_r[:, i.par], res)
            dve.wait_ge(res, base + 7)
            nc.vector.tensor_tensor(pair(x_all, i), pair(x_all, i), att[:, i.par], ALU.add).then_inc(res, 1)
            need(dve, post_rstd, NRSTD * (i.v - 2) + 4)
            dve_stats(tiles(x_all, i), st2, mv2[:, i.par], res, base + 8)

        def dve_slot(step, k):
            cur, nxt, nxt2, old, older, oldest = (item(step, d) for d in (0, 1, 2, -1, -2, -3))
            im, gm = group(step, k, 1)
            if k == 3 and nxt:
                dve.wait_ge(v_ps, nxt.v + 1)
                need(dve, pv_ps, 4 * (nxt.v - 2) + 4)
                for j in range(2):
                    m = nc.vector.tensor_tensor(
                        vaug[:, nxt.par, j, :, 0:HD],
                        mid_bank[:, j * P:(j + 1) * P].rearrange("p (h d) -> p h d", h=H),
                        bv_s[:, nxt.phase].rearrange("p (h d) -> p h d", h=H), ALU.add)
                m.then_inc(v_sb, 1)
            if k == 0 and oldest and oldest.phase == 1:
                dve.wait_ge(lg_ps, oldest.v - B + 1)
                nc.vector.tensor_tensor(pair(logits, oldest),
                                        mid_bank[:, 0:2 * E].rearrange("p (j e) -> p j e", j=2),
                                        gb_s[:, 0:1].to_broadcast([P, 2, E]), ALU.add).then_inc(lg_sb, 1)
            if k == 0 and older:
                dve_norm(older, 1)
            if k == 3 and older and older.phase == 2:
                dve.wait_ge(hT_sb, older.v - B + 1)
                nc.vector.tensor_reduce(hmean[:, bass.ds(older.b, 1)], hT[:, older.par], AX.X,
                                        ALU.add).then_inc(lg_sb, 1)
            if cur:
                dve_reduce(cur, k, 0)
            if im:
                dve_mT(im, gm)
            if k == 2 and older:
                dve_after(older)
            if k == 2 and nxt:
                dve_split(nxt)
            if cur:
                dve_reduce(cur, k, 1)
            if k == 1 and older:
                dve_residual(older)
            if k == 3 and old:
                dve_norm(old, 0)
            if cur:
                dve_reduce(cur, k, 2)
                dve_split_max(cur, k)
            if k == 3 and older and older.phase == 0:
                dve.wait_ge(post_rstd, NRSTD * older.v + NRSTD)
                dve_normal(tiles(f_all, older), tiles(x_all, older), mv2[:, older.par], r2[:, older.par], res)
            if k == 2 and nxt2:
                if nxt2.phase == 0:
                    dve.wait_ge(*((x_first, 16) if isinstance(nxt2.v, int) and nxt2.v < 4 else (x_rest, 16)))
                elif nxt2.phase == 1:
                    dve.wait_ge(res, NRES * (nxt2.v - B) + NRES)
                elif isinstance(nxt2.v, int) and nxt2.b == 0:
                    dve.wait_ge(b2_add, B)
                need(dve, pre_rstd, 2 * (nxt2.v - 2) + 2)
                dve_stats(tiles(x_all if nxt2.phase == 0 else f_all, nxt2), pre_st, pre_mv[:, nxt2.par],
                          pre_stats, NPRE * nxt2.v)
            if k == 3 and nxt2:
                dve.wait_ge(pre_rstd, 2 * nxt2.v + 2)
                need(dve, xT_ps, nxt2.v - 1)
                dve_normal([xn[:, nxt2.par, j] for j in range(2)],
                           tiles(x_all if nxt2.phase == 0 else f_all, nxt2), pre_mv[:, nxt2.par],
                           pre_r[:, nxt2.par], xn_ok)

        def pool_rstd(mv, r, s, base, last=1):
            alone(pool)
            nc.gpsimd.tensor_scalar(r, mv[:, :, 1], EPS, None, ALU.add).then_inc(s, 1)
            pool.wait_ge(s, base + 1)
            nc.gpsimd.tensor_tensor(r, r, power[:], ALU.pow).then_inc(s, last)

        def pool_select(i, g, u):
            pool.wait_ge(exp_done, unit(i, g, 2 * u))
            alone(pool)
            t = prob1[:, g % 2] if u == 0 else prob0[:, g % 2, :, 0:P]
            nc.gpsimd.affine_select(out=t, in_=t, compare_op=ALU.is_ge, fill=0.0, base=0,
                                    pattern=[[0, HG], [1, P]], channel_multiplier=-1).then_inc(sel_done, 1)

        def pool_slot(step, k):
            nxt2, older = item(step, 2), item(step, -2)
            ie, ge = group(step, k, 2)
            if k == 3 and nxt2:
                pool.wait_ge(pre_stats, NPRE * nxt2.v + 4)
                need(pool, xn_ok, 2 * (nxt2.v - 2) + 2)
                pool_rstd(pre_mv[:, nxt2.par], pre_r[:, nxt2.par], pre_rstd, 2 * nxt2.v)
            if k == 2 and older:
                pool.wait_ge(res, NRES * older.v + (5 if older.phase == 0 else 6))
                pool_rstd(post_mv[:, older.par], post_r[:, older.par], post_rstd, NRSTD * older.v,
                          1 if older.phase == 0 else NRSTD - 1)
            if k == 3 and older and older.phase == 0:
                pool.wait_ge(res, NRES * older.v + 12)
                pool_rstd(mv2[:, older.par], r2[:, older.par], post_rstd, NRSTD * older.v + 2)
            if ie:
                pool_select(ie, ge, 0)
                pool_select(ie, ge, 1)
            if k == 3 and older and older.phase > 0:
                pool.wait_ge(hT_sb, older.v - B + 1)
                nc.gpsimd.tensor_copy(hT_all[:, bass.ds(older.b * T, T)], hT[:, older.par]).then_inc(hT_kept, 1)

        def sp_slot(step, k):
            im, gm = group(step, k, 1)
            if im:
                sp.wait_ge(mT_sb, 4 * im.v + gm + 1)
                alone(sp)
                need(sp, sT_ps, 12 * (im.v - 2) + 3 * gm + 3)
                alone(sp)
                sp.dma_start(qstack[ROWS:SHIFT, im.par, HG * gm:HG * (gm + 1), :],
                             mT[:, gm % 2, :]).then_inc(row_dma[gm % 2], 16)
        block = ctx.enter_context(nc.Block())
        RUNS = [(0, 2 * B), (2 * B, 3 * B)]
        G0 = 19

        def dve_gate(layer):
            n = [G0 * layer]
            if layer == 0:
                dve.wait_ge(lg_sb, B)
                N, lg = NT, logits[:]
            else:
                N = B
                dve.wait_ge(lg_sb, 2 * B)
                spread = gtmp[:, 0, 0:B]
                nc.vector.tensor_tensor(spread, hmean[:].unsqueeze(2).to_broadcast([P, B, E]),
                                        gw_s[:, 1:2].to_broadcast([P, B, E]), ALU.mult).then_inc(gate_p, 1)
                dve.wait_ge(gate_p, 2)
                lg = logits[:, 0:B]
                nc.vector.scalar_tensor_tensor(out=lg, in0=pre_bank[:, 0:B * E].rearrange("p (b e) -> p b e", e=E),
                                               scalar=1.0 / T, in1=gb_s[:, 1:2].to_broadcast([P, B, E]),
                                               op0=ALU.mult, op1=ALU.add).then_inc(gate_p, 1)
                dve.wait_ge(gate_p, 3)

            def step(ins):
                n[0] += 1
                ins.then_inc(gate_v, 1)
                dve.wait_ge(gate_v, n[0])

            def wide(i):
                return gsm[:, i, 0:N].unsqueeze(2).to_broadcast([P, N, E])

            iota = iota_e[:].unsqueeze(1).to_broadcast([P, N, E])
            cur = lg
            for r in range(2):
                t, oh = gtmp[:, 1, 0:N], gtmp[:, 2 + r, 0:N]
                step(nc.vector.tensor_reduce(gsm[:, r, 0:N], cur, AX.X, ALU.max))
                step(nc.vector.tensor_tensor(t, cur, wide(r), ALU.is_equal))
                step(nc.vector.scalar_tensor_tensor(out=t, in0=t, scalar=-100.0, in1=iota, op0=ALU.mult,
                                                    op1=ALU.add))
                step(nc.vector.tensor_reduce(gsm[:, 2 + r, 0:N], t, AX.X, ALU.min))
                step(nc.vector.tensor_tensor(oh, t, wide(2 + r), ALU.is_equal))
                if r == 0:
                    step(nc.vector.scalar_tensor_tensor(out=gtmp[:, 4, 0:N], in0=oh, scalar=-3e38, in1=lg,
                                                        op0=ALU.mult, op1=ALU.add))
                    cur = gtmp[:, 4, 0:N]
            step(nc.vector.tensor_tensor(gsm[:, 4, 0:N], gsm[:, 1, 0:N], gsm[:, 0, 0:N], ALU.subtract))
            dve.wait_ge(gate_a, layer + 1)
            step(nc.vector.tensor_scalar(gsm[:, 6, 0:N], gsm[:, 5, 0:N], 1.0, None, ALU.add))
            step(nc.vector.reciprocal(gsm[:, 6, 0:N], gsm[:, 6, 0:N]))
            step(nc.vector.tensor_tensor(gsm[:, 5, 0:N], gsm[:, 5, 0:N], gsm[:, 6, 0:N], ALU.mult))
            if layer == 1:
                step(nc.vector.tensor_scalar(chosen[:], gsm[:, 2:4, 0:N], 100.0, None, ALU.add))
            step(nc.vector.tensor_tensor(gtmp[:, 2, 0:N], gtmp[:, 2, 0:N], wide(6), ALU.mult))
            step(nc.vector.tensor_tensor(gtmp[:, 3, 0:N], gtmp[:, 3, 0:N], wide(5), ALU.mult))
            nc.vector.tensor_tensor(cw[:, 0:N], gtmp[:, 2, 0:N], gtmp[:, 3, 0:N], ALU.add)\
              .then_inc(gate_v, G0 * (layer + 1) - n[0])
            dve.wait_ge(gate_v, G0 * (layer + 1))

        def act_gate(layer):
            act.wait_ge(gate_v, G0 * layer + 12)
            N = NT if layer == 0 else B
            nc.scalar.activation(gsm[:, 5, 0:N], gsm[:, 4, 0:N], ACT.Exp).then_inc(gate_a, 1)

        def pe_gate():
            pe.wait_ge(gate_p, 1)
            nc.tensor.matmul(pre_bank[:, 0:B * E], ones[:], gtmp[:, 0, 0:B].rearrange("p b e -> p (b e)"),
                             start=True, stop=True).then_inc(gate_p, 1)

        JOBS = (E, TOP)

        def jobs(layer, b):
            return B * E * layer + JOBS[layer] * b

        def pe_hidden(layer, b, e):
            j = jobs(layer, b) + e
            if layer == 1:
                pe.wait_ge(w1_got, j - B * E + 1)
            need(pe, gelu_done, FC * (j - 1))
            for c in range(FC):
                w = (w1_s, w1_job)[layer][:, e, c * P:(c + 1) * P]
                m = nc.tensor.matmul(bank[2 * (e % 2) + c // 2][:, (c % 2) * T:(c % 2 + 1) * T],
                                     w, hT_all[:, bass.ds(b * T, T)], start=True, stop=True)
                if c % 2:
                    m.then_inc(h_ps, 1)

        def pe_output(layer, b, e):
            j = jobs(layer, b) + e
            if layer == 1:
                pe.wait_ge(w2_got, j - B * E + 1)
            pe.wait_ge(gelu_done, FC * j + FC)
            need(pe, acc, 2 * (j - 1))
            for t in range(2):
                for c in range(FC):
                    m = nc.tensor.matmul(bank[4 + e % 2][:, t * P:(t + 1) * P],
                                         hid[:, e % 2, c, t * P:(t + 1) * P], (w2_s, w2_job)[layer][:, e, c],
                                         start=(c == 0), stop=(c == FC - 1))
            m.then_inc(y_ps, 1)

        def pe_experts(layer):
            tiles_of = (2, 1)[layer]

            def body(b, last):
                seq = b + B * layer
                for e in range(JOBS[layer]):
                    if e < JOBS[layer] - 1:
                        pe_hidden(layer, b, e + 1)
                    elif not last:
                        pe_hidden(layer, b + 1, 0)
                    if e == 0:
                        pe.wait_ge(cw_copied, seq + 1)
                        for t in range(tiles_of):
                            m = nc.tensor.transpose(bank[6][0:E, t * P:(t + 1) * P], cwt[:, t], ident[:])
                        m.then_inc(cwT_ps, 1)
                    if e == 1:
                        pe.wait_ge(cwT_sb, seq + 1)
                        need(pe, b2_add, seq)
                        for t in range(tiles_of):
                            m = nc.tensor.matmul(bank[7][:, t * P:(t + 1) * P], cwT[:, t * P:(t + 1) * P],
                                                 b2_s[:, layer], start=True, stop=True)
                        m.then_inc(b2_ps, 1)
                    pe_output(layer, b, e)

            pe.wait_ge(hT_kept, B * (layer + 1))
            pe.wait_ge(expert_ld[layer], 32)
            pe.wait_ge(gate_v, G0 * (layer + 1))
            pe_hidden(layer, 0, 0)
            body(0, False)
            with pe.Fori(1, B - 1) as b:
                body(b, False)
            body(B - 1, True)

        def act_experts(layer):
            def body(b):
                seq = b + B * layer
                for e in range(JOBS[layer]):
                    j = jobs(layer, b) + e
                    need(act, y_ps, j - 1)
                    if layer == 1:
                        act.wait_ge(w2_got, j - B * E + 1)
                    for c in range(FC):
                        if c % 2 == 0:
                            act.wait_ge(h_ps, 2 * j + c // 2 + 1)
                        bias = b1_s[:, 0, e, c:c + 1] if layer == 0 else b1_job[:, e, c:c + 1]
                        nc.scalar.activation(hid[:, e % 2, c],
                                             bank[2 * (e % 2) + c // 2][:, (c % 2) * T:(c % 2 + 1) * T],
                                             ACT.Gelu, bias=bias).then_inc(gelu_done, 1)
                    if e == 0:
                        act.wait_ge(cwT_ps, seq + 1)
                        need(act, b2_ps, seq)
                        nc.scalar.copy(cwT[:, 0:(2 - layer) * P], bank[6][0:E, 0:(2 - layer) * P])\
                          .then_inc(cwT_sb, 1)

            body(0)
            with act.Fori(1, B) as b:
                body(b)

        def dve_expert_w1(b, r):
            e = nc.vector.value_load(chosen[0:1, r, bass.ds(b, 1)], min_val=0, max_val=E - 1)
            need(dve, h_ps, 2 * jobs(1, b - 1) + 2 * r + 2 if not isinstance(b, int) or b > 0 else 0)
            alone(dve)
            nc.vector.tensor_copy(w1_job[:, r:r + 1], w1_s[:, bass.ds(e, 1)]).then_inc(w1_got, 1)
            return e

        def dve_expert_w2(b, r, e):
            need(dve, y_ps, jobs(1, b - 1) + r + 1 if not isinstance(b, int) or b > 0 else 0)
            alone(dve)
            nc.vector.tensor_copy(w2_job[:, r:r + 1], w2_s[:, bass.ds(e, 1)])
            nc.vector.tensor_copy(b1_job[:, r:r + 1], b1_s[:, 1, bass.ds(e, 1)]).then_inc(w2_got, 1)

        def dve_experts(layer):
            def body(b, last):
                seq = b + B * layer

                def weights(t):
                    at = 2 * b + t if layer == 0 else b
                    return cw[:, bass.ds(at, 1), :].rearrange("p a e -> p (a e)")

                need(dve, cwT_ps, seq)
                need(dve, acc, 2 * jobs(layer, b))
                for t in range(2 - layer):
                    m = nc.vector.tensor_copy(cwt[:, t], weights(t))
                if layer == 1:
                    for r in range(TOP):
                        m = nc.vector.tensor_copy(cwt[:, 1, r:r + 1], gsm[:, 6 - r, bass.ds(b, 1)])
                m.then_inc(cw_copied, 1)
                dve.wait_ge(cw_copied, seq + 1)
                for e in range(JOBS[layer]):
                    j = jobs(layer, b) + e
                    if layer == 1 and not last:
                        expert = dve_expert_w1(b + 1, e)
                    dve.wait_ge(y_ps, j + 1)
                    need(dve, acc, 2 * j)
                    for t in range(2):
                        f = f_all[:, bass.ds(2 * b + t, 1), :].rearrange("p a d -> p (a d)")
                        weight = cwt[:, t, e:e + 1] if layer == 0 else cwt[:, 1, e:e + 1]
                        nc.vector.scalar_tensor_tensor(out=f, in0=bank[4 + e % 2][:, t * P:(t + 1) * P],
                                                       scalar=weight, in1=f,
                                                       op0=ALU.mult, op1=ALU.add).then_inc(acc, 1)
                    if layer == 1 and not last:
                        dve_expert_w2(b + 1, e, expert)
                    if e == 1:
                        dve.wait_ge(b2_ps, seq + 1)
                        dve.wait_ge(acc, 2 * j + 2)
                        f = f_all[:, bass.ds(2 * b, 2), :]
                        y = bank[7][:, 0:(2 - layer) * P].rearrange("p (j d) -> p j d", d=P)
                        nc.vector.tensor_tensor(f, y if layer == 0 else y.to_broadcast([P, 2, P]), f,
                                                ALU.add).then_inc(b2_add, 1)
                        dve.wait_ge(b2_add, seq + 1)

            if layer == 1:
                dve.wait_ge(expert_ld[1], 32)
                for r in range(TOP):
                    dve_expert_w2(0, r, dve_expert_w1(0, r))
            body(0, False)
            with dve.Fori(1, B - 1) as b:
                body(b, False)
            body(B - 1, True)

        @block.sync
        def _(_):
            sp.dma_start(x_all[:, 0:8], x_dram[:, 0:8]).then_inc(x_first, 16)
            for t, d in ((wqk_s, w_qk), (bqk_s, b_qk), (ln1_s, ln1), (wv_s, w_v), (wo_s, w_o)):
                sp.dma_start(t[:], d).then_inc(small_ld, 16)
            sp.dma_start(x_all[:, 8:NT], x_dram[:, 8:NT]).then_inc(x_rest, 16)
            run_steps(sp, sp_slot, *RUNS[0])
            run_steps(sp, sp_slot, *RUNS[1])
            with sp.Fori(0, B) as b:
                sp.wait_ge(fin_x, b + 1)
                alone(sp)
                sp.dma_start(out_dram[:, bass.ds(2 * b, 2), :], x_all[:, bass.ds(2 * b, 2), :]).then_inc(out_dma, 16)
            sp.wait_ge(out_dma, 16 * B)

        @block.gpsimd
        def _(_):
            nc.gpsimd.memset(ident[:], 0.0).then_inc(const_ok, 1)
            nc.gpsimd.memset(maskneg[:], 0.0).then_inc(const_ok, 1)
            nc.gpsimd.memset(power[:], -0.5).then_inc(const_ok, 1)
            nc.gpsimd.iota(iota_e[:], pattern=[[1, E]], base=0, channel_multiplier=0,
                           allow_small_or_imprecise_dtypes=True).then_inc(const_ok, 1)
            pool.wait_ge(const_ok, 4)
            nc.gpsimd.affine_select(out=ident[:], in_=ident[:], compare_op=ALU.not_equal, fill=1.0, base=0,
                                    pattern=[[-1, P]], channel_multiplier=1).then_inc(const_ok, 1)
            nc.gpsimd.affine_select(out=maskneg[:], in_=maskneg[:], compare_op=ALU.is_ge, fill=MASKED, base=0,
                                    pattern=[[0, HG], [-1, P]], channel_multiplier=1).then_inc(const_ok, 1)
            pool.wait_ge(const_ok, 6)
            nc.gpsimd.tensor_copy(identb[:], ident[:]).then_inc(const_ok, 1)
            run_steps(pool, pool_slot, *RUNS[0])
            run_steps(pool, pool_slot, *RUNS[1])
            with pool.Fori(0, B - 1, 2) as n:
                for par in range(2):
                    pool.wait_ge(fin_v, 4 * (n + par) + 4)
                    pool_rstd(mv2[:, par], r2[:, par], fin_p, 2 * (n + par))

        @block.scalar
        def _(_):
            for t, d in ((bv_s, b_v), (bo_s, b_o), (gb_s, gate_b)):
                act.dma_start(t[:], d.partition_broadcast(P)).then_inc(small_ld, 16)
            for t, d in ((ln2_s, ln2), (gw_s, gate_w), (b1_s, e_b1), (b2_s, e_b2)):
                act.dma_start(t[:], d).then_inc(small_ld, 16)
            act.wait_ge(small_ld, SMALL)

            def load_experts(l):
                act.dma_start(w1_s[:], e_w1[l].rearrange("e d f -> d e f")).then_inc(expert_ld[l], 16)
                act.dma_start(w2_s[:].rearrange("p e c d -> p (e c) d"),
                              e_w2[l].rearrange("e (c p) d -> p (e c) d", p=P)).then_inc(expert_ld[l], 16)

            load_experts(0)
            run_steps(act, act_slot, *RUNS[0])
            act_gate(0)
            act_experts(0)
            act.wait_ge(y_ps, B * E)
            load_experts(1)
            run_steps(act, act_slot, *RUNS[1])
            act_gate(1)
            act_experts(1)

        @block.vector
        def _(_):
            nc.vector.memset(kstack[:], 1.0).then_inc(vconst_ok, 1)
            nc.vector.memset(vaug[:], 0.0).then_inc(vconst_ok, 1)
            dve.wait_ge(vconst_ok, 2)
            nc.vector.memset(vaug[:, :, :, :, HD:HD + 1], 1.0).then_inc(vconst_ok, 1)
            nc.vector.memset(ones[:], 1.0).then_inc(vconst_ok, 1)
            dve.wait_ge(small_ld, SMALL)
            run_steps(dve, dve_slot, *RUNS[0])
            dve_gate(0)
            dve_experts(0)
            run_steps(dve, dve_slot, *RUNS[1])
            dve_gate(1)
            dve_experts(1)
            dve.wait_ge(b2_add, 2 * B)
            def final(n):
                for par in range(2):
                    i = Item(n + par, par, 0)
                    dve_stats(tiles(f_all, i), st2, mv2[:, par], fin_v, 4 * i.v)
                for par in range(2):
                    i = Item(n + par, par, 0)
                    dve.wait_ge(fin_p, 2 * i.v + 2)
                    dve_normal([hn[:, par, j] for j in range(2)], tiles(f_all, i), mv2[:, par], r2[:, par], fin_n)
                    dve.wait_ge(fin_n, 2 * i.v + 2)
                    nc.vector.tensor_tensor(pair(x_all, i), pair(x_all, i), hn[:, par], ALU.add).then_inc(fin_x, 1)

            with dve.Fori(0, B - 1, 2) as n:
                final(n)

        @block.tensor
        def _(_):
            pe.wait_ge(const_ok, 7)
            pe.wait_ge(vconst_ok, 4)
            pe.wait_ge(small_ld, SMALL)
            run_steps(pe, pe_slot, *RUNS[0])
            pe_experts(0)
            run_steps(pe, pe_slot, *RUNS[1])
            pe_gate()
            pe_experts(1)



def kernel(**inputs):
    import concourse.bacc as bacc
    from concourse.bass_utils import run_bass_kernel_spmd

    a = {k: np.ascontiguousarray(v) for k, v in inputs.items()}
    f = {k[7:]: v for k, v in a.items() if k.startswith("L0_ffn_")}
    x, w_qkv, w_out = a["L0_attn_x"], a["L0_attn_w_qkv"], a["L0_attn_w_out"]
    zero, one = np.zeros(P, x.dtype), np.ones(P, x.dtype)

    def by_feature(w):
        return w.reshape(-1, H, HD).transpose(0, 2, 1).reshape(w.shape)

    def rows(vectors):
        return np.stack(vectors)

    def columns(vectors):
        return np.stack(vectors, axis=-1)

    qs = [w_qkv[:, 0:P], f["wq"][0], f["wq"][1]]
    ks = [w_qkv[:, P:2 * P], f["wk"][0], f["wk"][1]]
    vs = [w_qkv[:, 2 * P:], f["wv"][0], f["wv"][1]]
    os_ = [w_out, f["wo"][0], f["wo"][1]]
    arrays = {
        "x": x,
        "w_qk": np.stack([np.stack([by_feature(q), by_feature(k)], 1) for q, k in zip(qs, ks)], 1),
        "w_v": np.stack(vs, 1),
        "w_o": np.stack(os_, 1),
        "b_qk": np.stack([columns([by_feature(q[None])[0], by_feature(k[None])[0]])
                          for q, k in zip([zero, *f["bq"]], [zero, *f["bk"]])], 1),
        "b_v": rows([zero, *f["bv"]]),
        "b_o": rows([a["L0_attn_b_out"], *f["bo"]]),
        "ln1": np.stack([columns([w, b]) for w, b in zip([one, *f["ln1_w"]], [zero, *f["ln1_b"]])], 1),
        "ln2": np.stack([columns([w, b]) for w, b in zip(f["ln2_w"], f["ln2_b"])], 1),
        "gate_w": f["gate_w"].transpose(1, 0, 2),
        "gate_b": f["gate_b"],
        "e_w1": f["e_w1"],
        "e_b1": f["e_b1"].reshape(2, E, -1, P).transpose(3, 0, 1, 2),
        "e_w2": f["e_w2"],
        "e_b2": f["e_b2"].transpose(1, 0, 2),
    }
    arrays = {k: np.ascontiguousarray(v) for k, v in arrays.items()}
    nc = bacc.Bacc("TRN2", target_bir_lowering=False, num_devices=1)
    args = [nc.dram_tensor(k, v.shape, mybir.dt.from_np(v.dtype), kind="ExternalInput").ap()
            for k, v in arrays.items()]
    out = nc.dram_tensor("out", x.shape, F32, kind="ExternalOutput").ap()
    build(nc, *args, out)
    r = run_bass_kernel_spmd(nc, [arrays], core_ids=[0])
    return r.results[0]["out"]
```

```python
from contextlib import ExitStack

import numpy as np

import concourse.bass as bass
from concourse import mybir

ALU = mybir.AluOpType
ACT = mybir.ActivationFunctionType
AX = mybir.AxisListType
F32 = mybir.dt.float32
BF16 = mybir.dt.bfloat16
I32 = mybir.dt.int32

P = 128
H = 16
HD = P // H
HG = 4
NG = H // HG
E = 8
TOP = 2
EPS = 1e-5
SCALE = float(HD) ** -0.5
MASKED = -1e30
TERM = [(0, 0), (0, 1), (0, 2), (1, 0), (1, 1), (2, 0)]
TERMS = len(TERM)
ROWS = TERMS * HD
SHIFT = P - 2
NPRE, NRSTD, NRES, NSPLIT = 4, 4, 14, 3
STACK_DMAS = TERMS


def need(eng, sem, value):
    if isinstance(value, int) and value <= 0:
        return
    eng.wait_ge(sem, value)


def build(nc, x_in, w_qk, w_v, w_o, b_qk, b_v, b_o, ln1, ln2, gate_w, gate_b, e_w1, e_b1, e_w2, e_b2, out):
    B, T, D = x_in.shape
    assert D == P and T == 2 * P and B % 2 == 0 and B >= 8
    L, _, _, DFF = e_w1.shape
    FC = DFF // P
    NT = B * 2

    pe, act, dve, pool, sp = nc.tensor, nc.scalar, nc.vector, nc.gpsimd, nc.sync

    with ExitStack() as ctx:
        def sb(name, shape, dt=F32):
            return ctx.enter_context(nc.sbuf_tensor(name, shape, dt))

        def sem(name):
            return ctx.enter_context(nc.semaphore(name))

        bank = [ctx.enter_context(nc.psum_tensor(f"bank{i}", [P, 512], F32)) for i in range(8)]
        max_bank, exp_bank = bank[0:2], bank[2:4]
        pv_bank, pre_bank, mid_bank, post_bank = bank[4:8]
        v_bank, lg_bank = post_bank[:, 0:T], post_bank[:, T:T + 2 * E]

        x_all = sb("x_all", [P, NT, P])
        f_all = sb("f_all", [P, NT, P])
        hT_all = sb("hT_all", [P, NT * P])
        wqk_s = sb("wqk_s", [P, 3, 2, P])
        wv_s = sb("wv_s", [P, 3, P])
        wo_s = sb("wo_s", [P, 3, P])
        bqk_s = sb("bqk_s", [P, 3, 2])
        bv_s = sb("bv_s", [P, 3, P])
        bo_s = sb("bo_s", [P, 3, P])
        ln1_s = sb("ln1_s", [P, 3, 2])
        ln2_s = sb("ln2_s", [P, L, 2])
        gw_s = sb("gw_s", [P, L, E])
        gb_s = sb("gb_s", [P, L, E])
        w1_s = sb("w1_s", [P, E, DFF])
        w2_s = sb("w2_s", [P, E, FC, P])
        b1_s = sb("b1_s", [P, L, E, FC])
        b2_s = sb("b2_s", [E, L, P])
        ident = sb("ident", [P, P])
        identb = sb("identb", [P, P], BF16)
        maskneg = sb("maskneg", [P, HG, P], BF16)
        ones = sb("ones", [P, P])
        power = sb("power", [P, 2])
        iota_e = sb("iota_e", [P, E])
        pre_st = sb("pre_st", [P, 2, 6])
        pre_mv = sb("pre_mv", [P, 2, 2, 2])
        pre_r = sb("pre_r", [P, 2, 2])
        xn = sb("xn", [P, 2, 2, P])
        xT = sb("xT", [P, 2, T])
        qkf = sb("qkf", [P, 2, T])
        rest = sb("rest", [P, 2, T])
        parts = sb("parts", [P, 2, 2, 3, T], BF16)
        stack = sb("stack", [P, 2, H, 2, T], BF16)
        vaug = sb("vaug", [P, 2, 2, H, 32])
        negm = sb("negm", [P, 2, 2, HG])
        mparts = sb("mparts", [P, 2, 2, 2, HG], BF16)
        mT = sb("mT", [2 * HG, 2, T], BF16)
        prob1 = sb("prob1", [P, 2, HG, P])
        prob0 = sb("prob0", [P, 2, HG, T])
        oT = sb("oT", [P, 2, NG, T])
        rden = sb("rden", [P, 2, H])
        on = sb("on", [P, 2, 2, P])
        onT = sb("onT", [P, 2, T])
        att = sb("att", [P, 2, 2, P])
        post_st = sb("post_st", [P, 2, 6])
        post_mv = sb("post_mv", [P, 2, 2, 2])
        post_r = sb("post_r", [P, 2, 2])
        st2 = sb("st2", [P, 2, 6])
        mv2 = sb("mv2", [P, 2, 2, 2])
        r2 = sb("r2", [P, 2, 2])
        hn = sb("hn", [P, 2, 2, P])
        hT = sb("hT", [P, 2, T])
        logits = sb("logits", [P, NT, E])
        hmean = sb("hmean", [P, B])
        gtmp = sb("gtmp", [P, 5, NT, E])
        gsm = sb("gsm", [P, 7, NT])
        cw = sb("cw", [P, NT, E])
        hid = prob0
        cwt = sb("cwt", [P, 2, E])
        cwT = sb("cwT", [E, T])
        chosen = sb("chosen", [P, TOP, B], I32)
        w1_job = sb("w1_job", [P, TOP, DFF])
        w2_job = sb("w2_job", [P, TOP, FC, P])
        b1_job = sb("b1_job", [P, TOP, FC])

        const_ok, waited = sem("const_ok"), sem("waited")
        vconst_ok, qstack_ok = sem("vconst_ok"), sem("qstack_ok")
        x_first, x_rest = sem("x_first"), sem("x_rest")
        small_ld = sem("small_ld")
        expert_ld = [sem("expert_ld0"), sem("expert_ld1")]
        pre_stats, pre_rstd, xn_ok = sem("pre_stats"), sem("pre_rstd"), sem("xn_ok")
        xT_ps, xT_sb, qk_ps, v_ps = sem("xT_ps"), sem("xT_sb"), sem("qk_ps"), sem("v_ps")
        qkf_sb, split, v_sb = sem("qkf_sb"), sem("split"), sem("v_sb")
        stack_dma = [sem("stack_dma0"), sem("stack_dma1")]
        row_dma = [sem("row_dma0"), sem("row_dma1")]
        max_ps, max_done, negmax = sem("max_ps"), sem("max_done"), sem("negmax")
        maxT_ps, mT_sb = sem("maxT_ps"), sem("mT_sb")
        sT_ps, exp_done, sel_done, pv_ps, ot_sb = sem("sT_ps"), sem("exp_done"), sem("sel_done"), sem("pv_ps"), sem("ot_sb")
        o1_ps, attn_n, o2_ps, onT_sb, o3_ps = sem("o1_ps"), sem("attn_n"), sem("o2_ps"), sem("onT_sb"), sem("o3_ps")
        res, post_rstd = sem("res"), sem("post_rstd")
        hT_ps, hT_sb, hT_kept, lg_ps, lg_sb = sem("hT_ps"), sem("hT_sb"), sem("hT_kept"), sem("lg_ps"), sem("lg_sb")
        gate_v, gate_a, gate_p = sem("gate_v"), sem("gate_a"), sem("gate_p")
        h_ps, gelu_done, y_ps, acc = sem("h_ps"), sem("gelu_done"), sem("y_ps"), sem("acc")
        w1_got, w2_got = sem("w1_got"), sem("w2_got")
        cw_copied, cwT_ps, cwT_sb, b2_ps, b2_add = sem("cw_copied"), sem("cwT_ps"), sem("cwT_sb"), sem("b2_ps"), sem("b2_add")
        fin_v, fin_p, fin_n, fin_x, out_dma = sem("fin_v"), sem("fin_p"), sem("fin_n"), sem("fin_x"), sem("out_dma")

        SMALL = 12 * 16
        x_dram = x_in.rearrange("b (j p) d -> p (b j) d", p=P)
        out_dram = out.rearrange("b (j p) d -> p (b j) d", p=P)

        class Item:
            def __init__(self, v, par, phase):
                self.v, self.par, self.phase = v, par, phase
                self.b = v - phase * B

        def item(step, d):
            n, par, phase, lo, hi = step
            if isinstance(n, int):
                v = n + d
                return Item(v, v % 2, v // B) if lo <= v < hi else None
            return Item(n + d, (par + d) % 2, phase)

        def group(step, k, lag):
            d, g = divmod(k - lag, NG)
            return item(step, d), g

        def run_steps(eng, slot, lo, hi):
            def peeled(a, b):
                for n in range(a, b):
                    for k in range(NG):
                        slot((n, n % 2, None, lo, hi), k)

            at = lo - 2
            for phase in range(lo // B, hi // B):
                first, last = phase * B + 4, phase * B + B - 2
                peeled(at, first)
                with eng.Fori(first, last - 1, 2) as n:
                    for d in range(2):
                        for k in range(NG):
                            slot((n + d, d, phase, lo, hi), k)
                at = last
            peeled(at, hi + 3)

        def alone(eng):
            eng.sem_inc(waited, 1)

        def unit(i, g, u):
            return 12 * i.v + 3 * g + u + 1

        def stack_ready(i):
            return 8 * STACK_DMAS * (i.v + (2 if i.par == 0 else 1))

        def rows_ready(i, g):
            return 32 * i.v + 16 * (g // 2 + 1)

        def pe_max(i, g, u):
            p0 = HG * g
            if g == 0 and u == 0:
                pe.wait_ge(stack_dma[i.par], stack_ready(i))
            need(pe, max_done, unit(i, g, u) - 2)
            bk = max_bank[(g + u) % 2]
            q, k = stack[0:SHIFT, i.par, :, 0], stack[0:SHIFT, i.par, :, 1]
            if u == 0:
                o = bk[:].rearrange("p (h k) -> p h k", h=HG)
                nc.tensor.matmul(o, identb[:], maskneg[:], start=True, stop=False, skip_group_check=True)
                for h in range(HG):
                    m = nc.tensor.matmul(o[:, h], q[:, p0 + h, 0:P], k[:, p0 + h, 0:P],
                                         start=False, stop=True, skip_group_check=True)
            else:
                o = bk[:].rearrange("p (h k) -> p h k", h=2)
                nc.tensor.matmul(o[:, :, P:T], identb[:], maskneg[:, 0:2], start=True, stop=False,
                                 skip_group_check=True)
                for h in range(2):
                    hh = p0 + 2 * (u - 1) + h
                    m = nc.tensor.matmul(o[:, h], q[:, hh, P:T], k[:, hh, :],
                                         start=False, stop=True, skip_group_check=True)
            m.then_inc(max_ps, 1)

        def pe_scores(i, g, u):
            p0 = HG * g
            if u == 0:
                pe.wait_ge(row_dma[g % 2], rows_ready(i, g))
            need(pe, exp_done, unit(i, g, u) - 2)
            bk = exp_bank[(g + u) % 2]
            q, k = stack[:, i.par, :, 0], stack[:, i.par, :, 1]
            if u == 0:
                for h in range(HG):
                    m = nc.tensor.matmul(bk[:, h * P:(h + 1) * P], k[:, p0 + h, P:T], q[:, p0 + h, P:T],
                                         start=True, stop=True)
            else:
                for h in range(2):
                    hh = p0 + 2 * (u - 1) + h
                    m = nc.tensor.matmul(bk[:, h * T:(h + 1) * T], k[:, hh, 0:P], q[:, hh, :],
                                         start=True, stop=True)
            m.then_inc(sT_ps, 1)

        def pe_values(i, g, half):
            G = 4 * i.v + g
            if half == 0:
                need(pe, v_sb, i.v + 1)
                pe.wait_ge(sel_done, 2 * G + 2)
                need(pe, ot_sb, G)
            for h in range(2 * half, 2 * half + 2):
                head = HG * g + h
                o = pv_bank[32 * h:32 * h + 32, 0:T]
                nc.tensor.matmul(o, vaug[:, i.par, 0, head], prob0[:, g % 2, h], start=True, stop=False,
                                 skip_group_check=True)
                m = nc.tensor.matmul(o[:, P:T], vaug[:, i.par, 1, head], prob1[:, g % 2, h],
                                     start=False, stop=True, skip_group_check=True)
            if half == 1:
                m.then_inc(pv_ps, 1)

        def pe_max_T(i, g):
            G = 4 * i.v + g
            pe.wait_ge(negmax, 2 * G + 2)
            need(pe, mT_sb, G)
            o = mid_bank[0:2 * HG, 0:P].bitcast(BF16)
            for qb in range(2):
                m = nc.tensor.transpose(o[:, qb * P:(qb + 1) * P],
                                        mparts[:, g % 2, qb].rearrange("p a h -> p (a h)"), identb[:])
            m.then_inc(maxT_ps, 1)

        def pe_xT(i):
            pe.wait_ge(xn_ok, 2 * i.v + 2)
            need(pe, qkf_sb, 4 * i.v)
            for j in range(2):
                m = nc.tensor.transpose(pre_bank[:, j * P:(j + 1) * P], xn[:, i.par, j], ident[:])
            m.then_inc(xT_ps, 1)

        def pe_qk(i):
            pe.wait_ge(xT_sb, i.v + 1)
            if i.v - 4 >= B if isinstance(i.v, int) else i.phase > 0:
                pe.wait_ge(hT_sb, i.v - 4 - B + 1)
            for t in range(2):
                m = nc.tensor.matmul(pre_bank[:, t * T:(t + 1) * T], wqk_s[:, i.phase, t], xT[:, i.par],
                                     start=True, stop=True)
            m.then_inc(qk_ps, 1)

        def pe_v(i):
            for j in range(2):
                m = nc.tensor.matmul(v_bank[:, j * P:(j + 1) * P], xT[:, i.par, j * P:(j + 1) * P],
                                     wv_s[:, i.phase], start=True, stop=True)
            m.then_inc(v_ps, 1)

        def pe_o1(i, qb):
            if qb == 0:
                pe.wait_ge(ot_sb, 4 * i.v + 4)
                need(pe, res, NRES * (i.v - 1) + 1)
            else:
                pe.wait_ge(attn_n, 4 * i.v + 2)
            for g in range(NG):
                m = nc.tensor.transpose(post_bank[:, g * P:(g + 1) * P], oT[:, i.par, g, qb * P:(qb + 1) * P],
                                        ident[:])
            m.then_inc(o1_ps, 1)

        def pe_o2(i):
            pe.wait_ge(attn_n, 4 * i.v + 4)
            for qb in range(2):
                m = nc.tensor.transpose(post_bank[:, qb * P:(qb + 1) * P], on[:, i.par, qb], ident[:])
            m.then_inc(o2_ps, 1)

        def pe_o3(i):
            pe.wait_ge(onT_sb, i.v + 1)
            for qb in range(2):
                m = nc.tensor.matmul(post_bank[:, qb * P:(qb + 1) * P], onT[:, i.par, qb * P:(qb + 1) * P],
                                     wo_s[:, i.phase], start=True, stop=True)
            m.then_inc(o3_ps, 1)

        def pe_hT(i):
            pe.wait_ge(res, NRES * i.v + NRES)
            end = (2 if i.v < 2 * B else 3) * B if isinstance(i.v, int) else None
            pe.wait_ge(qkf_sb, 4 * (min(i.v + 4, end) if end else i.v + 4))
            for j in range(2):
                m = nc.tensor.transpose(pre_bank[:, T + j * P:T + (j + 1) * P], hn[:, i.par, j], ident[:])
            m.then_inc(hT_ps, 1)

        def pe_logits(i):
            pe.wait_ge(hT_sb, i.v - B + 1)
            need(pe, lg_sb, i.v - B)
            for j in range(2):
                m = nc.tensor.matmul(lg_bank[:, j * E:(j + 1) * E], hT[:, i.par, j * P:(j + 1) * P],
                                     gw_s[:, 0], start=True, stop=True)
            m.then_inc(lg_ps, 1)

        def pe_slot(step, k):
            cur, nxt, nxt2, old, older, oldest = (item(step, d) for d in (0, 1, 2, -1, -2, -3))
            (ie, ge), (iv, gv), (im, gm) = group(step, k, 2), group(step, k, 3), group(step, k, 1)
            if cur:
                pe_max(cur, k, 0)
            if ie:
                pe_scores(ie, ge, 0)
            if k == 0 and nxt:
                pe_qk(nxt)
            if k == 3 and old:
                if nxt:
                    pe.wait_ge(v_sb, nxt.v + 1)
                if oldest and oldest.phase == 1:
                    pe.wait_ge(lg_sb, oldest.v - B + 1)
                pe_o1(old, 0)
            if im:
                pe_max_T(im, gm)
            if cur:
                pe_max(cur, k, 1)
            if ie:
                pe_scores(ie, ge, 1)
            if iv:
                pe_values(iv, gv, 0)
            if k == 0 and older:
                pe_o2(older)
            if k == 3 and older and older.phase > 0:
                pe_hT(older)
            if cur:
                pe_max(cur, k, 2)
            if ie:
                pe_scores(ie, ge, 2)
            if iv:
                pe_values(iv, gv, 1)
            if k == 0 and older:
                pe_o3(older)
            if k == 1 and older and (nxt or oldest and oldest.phase == 1):
                pe.wait_ge(res, NRES * older.v + 1)
            if k == 1 and oldest and oldest.phase == 1:
                pe_logits(oldest)
            if k == 1 and nxt:
                pe_v(nxt)
            if k == 3 and older and older.phase > 0 and nxt2:
                pe.wait_ge(hT_sb, older.v - B + 1)
            if k == 3 and nxt2:
                pe_xT(nxt2)
            if k == 3 and old:
                pe_o1(old, 1)

        def act_exp(i, g, u):
            act.wait_ge(sT_ps, unit(i, g, u))
            if u == 0:
                need(act, pv_ps, 4 * i.v + g - 1)
            bk = exp_bank[(g + u) % 2]
            if u == 0:
                o, s = prob1[:, g % 2].rearrange("p h q -> p (h q)"), bk[:]
            else:
                o, s = prob0[:, g % 2, 2 * u - 2:2 * u].rearrange("p h q -> p (h q)"), bk[:]
            nc.scalar.activation(o, s, ACT.Exp, scale=SCALE).then_inc(exp_done, 1)

        def act_oT(i, g):
            act.wait_ge(pv_ps, 4 * i.v + g + 1)
            if g == 0:
                need(act, o1_ps, 2 * (i.v - 2) + 2)
            nc.scalar.copy(oT[:, i.par, g], pv_bank[:, 0:T]).then_inc(ot_sb, 1)

        def act_qk(i, t):
            if t == 0:
                act.wait_ge(qk_ps, i.v + 1)
                need(act, split, NSPLIT * (i.v - 1) + 1)
                need(act, stack_dma[i.par], stack_ready(i) - 16 * STACK_DMAS)
            for o in (qkf[:, t], parts[:, i.par, t, 0]):
                nc.scalar.activation(o, pre_bank[:, t * T:(t + 1) * T], ACT.Identity,
                                     bias=bqk_s[:, i.phase, t:t + 1]).then_inc(qkf_sb, 1)

        def act_part(i):
            act.wait_ge(split, NSPLIT * i.v + 1)
            nc.scalar.copy(parts[:, i.par, :, 1], rest[:]).then_inc(split, 1)

        def act_slot(step, k):
            cur, nxt, nxt2, old, older = (item(step, d) for d in (0, 1, 2, -1, -2))
            (ie, ge), (io, go) = group(step, k, 2), group(step, k, 4)
            if io:
                act_oT(io, go)
            if ie:
                act_exp(ie, ge, 0)
            if ie:
                act_exp(ie, ge, 1)
            if k == 0 and nxt:
                act_qk(nxt, 0)
            if k == 1 and nxt:
                act_part(nxt)
            if k == 0 and older:
                act.wait_ge(o2_ps, older.v + 1)
                need(act, o3_ps, older.v - 1)
                nc.scalar.copy(onT[:, older.par], post_bank[:, 0:T]).then_inc(onT_sb, 1)
            if ie:
                act_exp(ie, ge, 2)
            if k == 0 and nxt:
                act_qk(nxt, 1)
            if k == 3 and older and older.phase > 0:
                act.wait_ge(hT_ps, older.v - B + 1)
                need(act, hT_kept, older.v - B - 1)
                if older.phase == 1:
                    need(act, lg_ps, older.v - B - 1)
                else:
                    need(act, lg_sb, older.v - B - 1)
                nc.scalar.activation(hT[:, older.par], pre_bank[:, T:2 * T], ACT.Identity,
                                     scale=ln2_s[:, older.phase - 1, 0:1], bias=ln2_s[:, older.phase - 1, 1:2])\
                  .then_inc(hT_sb, 1)
            if k == 3 and nxt2:
                act.wait_ge(xT_ps, nxt2.v + 1)
                need(act, v_ps, nxt2.v - 1)
                nc.scalar.activation(xT[:, nxt2.par], pre_bank[:, 0:T], ACT.Identity,
                                     scale=ln1_s[:, nxt2.phase, 0:1], bias=ln1_s[:, nxt2.phase, 1:2])\
                  .then_inc(xT_sb, 1)

        def dve_reduce(i, g, u):
            dve.wait_ge(max_ps, unit(i, g, u))
            if u == 0:
                need(dve, negmax, 2 * (4 * i.v + g) - 2)
            bk = max_bank[(g + u) % 2]
            if u == 0:
                o, s = negm[:, g % 2, 0], bk[:].rearrange("p (h k) -> p h k", h=HG)
            else:
                o, s = negm[:, g % 2, 1, 2 * u - 2:2 * u], bk[:].rearrange("p (h k) -> p h k", h=2)
            nc.vector.tensor_reduce(o, s, AX.X, ALU.max, negate=True).then_inc(max_done, 1)

        def dve_split_max(i, g):
            G = 4 * i.v + g
            dve.wait_ge(max_done, unit(i, g, 2))
            need(dve, maxT_ps, G - 1)
            nc.vector.tensor_copy(mparts[:, g % 2, :, 0], negm[:, g % 2]).then_inc(negmax, 1)
            dve.wait_ge(negmax, 2 * G + 1)
            nc.vector.tensor_tensor(mparts[:, g % 2, :, 1], negm[:, g % 2], mparts[:, g % 2, :, 0],
                                    ALU.subtract).then_inc(negmax, 1)

        def dve_mT(i, g):
            dve.wait_ge(maxT_ps, 4 * i.v + g + 1)
            need(dve, row_dma[g % 2], rows_ready(i, g) - 16)
            nc.vector.tensor_copy(mT[:, g % 2], mid_bank[0:2 * HG, 0:P].bitcast(BF16)).then_inc(mT_sb, 1)

        def dve_norm(i, qb):
            dve.wait_ge(o1_ps, 2 * i.v + qb + 1)
            o = post_bank[:].rearrange("p (h c) -> p h c", c=32)
            need(dve, o2_ps, i.v - 1)
            nc.vector.reciprocal(rden[:, qb], o[:, :, HD]).then_inc(attn_n, 1)
            dve.wait_ge(attn_n, 4 * i.v + 2 * qb + 1)
            nc.vector.tensor_tensor(on[:, i.par, qb].rearrange("p (h d) -> p h d", d=HD), o[:, :, 0:HD],
                                    rden[:, qb].unsqueeze(2).to_broadcast([P, H, HD]),
                                    ALU.mult).then_inc(attn_n, 1)

        def dve_stats(src, st, s, base):
            need(dve, s, base)
            alone(dve)
            for j in range(2):
                nc.vector.bn_stats(st[:, j], src[j]).then_inc(s, 1)

        def dve_moments(st, mv, s, base):
            dve.wait_ge(s, base + 2)
            alone(dve)
            for j in range(2):
                nc.vector.bn_aggr(mv[:, j], st[:, j]).then_inc(s, 1)

        def tiles(t, i):
            return [t[:, bass.ds(2 * i.b + j, 1), :].rearrange("p a d -> p (a d)") for j in range(2)]

        def pair(t, i):
            return t[:, bass.ds(2 * i.b, 2), :]

        def dve_normal(dst, src, mv, r, s, last=1):
            for j in range(2):
                nc.vector.tensor_scalar(dst[j], src[j], mv[:, j, 0:1], r[:, j:j + 1],
                                        ALU.subtract, ALU.mult).then_inc(s, last if j else 1)

        def dve_residual(i):
            base = NRES * i.v
            dve.wait_ge(o3_ps, i.v + 1)
            nc.vector.tensor_tensor(att[:, i.par], post_bank[:, 0:T].rearrange("p (j d) -> p j d", j=2),
                                    bo_s[:, i.phase:i.phase + 1].to_broadcast([P, 2, P]),
                                    ALU.add).then_inc(res, 1)
            if i.phase > 0:
                dve.wait_ge(res, base + 1)
                nc.vector.tensor_tensor(pair(f_all, i), pair(f_all, i), att[:, i.par], ALU.add).then_inc(res, 1)

        def summed(i):
            return NRES * i.v + (2 if i.phase > 0 else 1)

        def dve_residual_stats(i):
            src = tiles(f_all, i) if i.phase > 0 else [att[:, i.par, j] for j in range(2)]
            dve_stats(src, post_st, res, summed(i))

        def dve_residual_moments(i):
            need(dve, post_rstd, NRSTD * (i.v - 2) + 2)
            dve_moments(post_st, post_mv[:, i.par], res, summed(i))

        def dve_normalise(i):
            dve.wait_ge(post_rstd, NRSTD * i.v + (2 if i.phase == 0 else NRSTD))
            if i.phase > 0:
                need(dve, hT_ps, i.v - B - 1)
                dve_normal([hn[:, i.par, j] for j in range(2)], tiles(f_all, i), post_mv[:, i.par],
                           post_r[:, i.par], res, NRES - 7)
            else:
                att_j = [att[:, i.par, j] for j in range(2)]
                dve_normal(att_j, att_j, post_mv[:, i.par], post_r[:, i.par], res)

        def dve_x(i):
            dve.wait_ge(res, NRES * i.v + 7)
            nc.vector.tensor_tensor(pair(x_all, i), pair(x_all, i), att[:, i.par], ALU.add).then_inc(res, 1)

        def dve_f(i):
            dve.wait_ge(post_rstd, NRSTD * i.v + NRSTD)
            dve_normal(tiles(f_all, i), tiles(x_all, i), mv2[:, i.par], r2[:, i.par], res)

        def dve_values(i):
            dve.wait_ge(v_ps, i.v + 1)
            need(dve, pv_ps, 4 * (i.v - 2) + 4)
            for j in range(2):
                m = nc.vector.tensor_tensor(vaug[:, i.par, j, :, 0:HD],
                                            v_bank[:, j * P:(j + 1) * P].rearrange("p (h d) -> p h d", h=H),
                                            bv_s[:, i.phase].rearrange("p (h d) -> p h d", h=H), ALU.add)
            m.then_inc(v_sb, 1)

        def dve_logits(i):
            dve.wait_ge(lg_ps, i.v - B + 1)
            nc.vector.tensor_tensor(pair(logits, i), lg_bank.rearrange("p (j e) -> p j e", j=2),
                                    gb_s[:, 0:1].to_broadcast([P, 2, E]), ALU.add).then_inc(lg_sb, 1)

        def dve_mean(i):
            dve.wait_ge(hT_sb, i.v - B + 1)
            nc.vector.tensor_reduce(hmean[:, bass.ds(i.b, 1)], hT[:, i.par], AX.X, ALU.add).then_inc(lg_sb, 1)

        def dve_input(i):
            if i.phase == 0:
                dve.wait_ge(*((x_first, 16) if isinstance(i.v, int) and i.v < 4 else (x_rest, 16)))
            elif i.phase == 1:
                dve.wait_ge(res, NRES * (i.v - B) + NRES)
            elif isinstance(i.v, int) and i.b == 0:
                dve.wait_ge(b2_add, B)
            return tiles(x_all if i.phase == 0 else f_all, i)

        def dve_slot(step, k):
            cur, nxt, nxt2, old, older, oldest = (item(step, d) for d in (0, 1, 2, -1, -2, -3))
            im, gm = group(step, k, 1)
            if cur:
                dve_reduce(cur, k, 0)
            if im:
                dve_mT(im, gm)
            if k == 0 and older:
                dve_norm(older, 1)
            if k == 1 and older:
                dve_residual(older)
            if k == 2 and nxt2:
                need(dve, pre_rstd, 2 * (nxt2.v - 2) + 2)
                dve_moments(pre_st, pre_mv[:, nxt2.par], pre_stats, NPRE * nxt2.v)
            if k == 3 and nxt2:
                dve.wait_ge(pre_rstd, 2 * nxt2.v + 2)
                need(dve, xT_ps, nxt2.v - 1)
                dve_normal([xn[:, nxt2.par, j] for j in range(2)], tiles(x_all if nxt2.phase == 0 else f_all, nxt2),
                           pre_mv[:, nxt2.par], pre_r[:, nxt2.par], xn_ok)
            if cur:
                dve_reduce(cur, k, 1)
            if k == 1 and older:
                dve_residual_stats(older)
            if k == 2 and older:
                dve_normalise(older)
            if k == 3 and older and older.phase == 0:
                dve_stats(tiles(x_all, older), st2, res, NRES * older.v + 8)
            if k == 3 and old:
                dve_norm(old, 0)
            if k == 0 and oldest and oldest.phase == 2:
                dve_mean(oldest)
            if cur:
                dve_reduce(cur, k, 2)
                dve_split_max(cur, k)
            if k == 0 and oldest and oldest.phase == 0:
                dve_f(oldest)
            if k == 2 and nxt:
                dve_values(nxt)
            if k == 2 and oldest and oldest.phase == 1:
                dve_logits(oldest)
            if k == 1 and older:
                dve_residual_moments(older)
            if k == 1 and nxt2:
                dve_stats(dve_input(nxt2), pre_st, pre_stats, NPRE * nxt2.v)
            if k == 2 and older and older.phase == 0:
                dve_x(older)
            if k == 3 and older and older.phase == 0:
                need(dve, post_rstd, NRSTD * (older.v - 2) + 4)
                dve_moments(st2, mv2[:, older.par], res, NRES * older.v + 8)
        def pool_rstd(mv, r, s, base, last=1):
            alone(pool)
            nc.gpsimd.tensor_scalar(r, mv[:, :, 1], EPS, None, ALU.add).then_inc(s, 1)
            pool.wait_ge(s, base + 1)
            nc.gpsimd.tensor_tensor(r, r, power[:], ALU.pow).then_inc(s, last)

        def pool_select(i, g, u):
            pool.wait_ge(exp_done, unit(i, g, 2 * u))
            alone(pool)
            t = prob1[:, g % 2] if u == 0 else prob0[:, g % 2, :, 0:P]
            nc.gpsimd.affine_select(out=t, in_=t, compare_op=ALU.is_ge, fill=0.0, base=0,
                                    pattern=[[0, HG], [1, P]], channel_multiplier=-1).then_inc(sel_done, 1)

        def pool_rest(i):
            base = NSPLIT * i.v
            pool.wait_ge(qkf_sb, 4 * i.v + 4)
            need(pool, split, base)
            alone(pool)
            nc.gpsimd.tensor_tensor(rest[:], qkf[:], parts[:, i.par, :, 0], ALU.subtract).then_inc(split, 1)

        def pool_part(i):
            pool.wait_ge(split, NSPLIT * i.v + 2)
            alone(pool)
            nc.gpsimd.tensor_tensor(parts[:, i.par, :, 2], rest[:], parts[:, i.par, :, 1],
                                    ALU.subtract).then_inc(split, 1)

        def pool_slot(step, k):
            nxt, nxt2, older, oldest = (item(step, d) for d in (1, 2, -2, -3))
            ie, ge = group(step, k, 2)
            if k == 2 and older:
                pool.wait_ge(res, summed(older) + 4)
                pool_rstd(post_mv[:, older.par], post_r[:, older.par], post_rstd, NRSTD * older.v,
                          1 if older.phase == 0 else NRSTD - 1)
            if k == 0 and oldest and oldest.phase == 0:
                pool.wait_ge(res, NRES * oldest.v + 12)
                pool_rstd(mv2[:, oldest.par], r2[:, oldest.par], post_rstd, NRSTD * oldest.v + 2)
            if ie:
                pool_select(ie, ge, 0)
            if k == 2 and nxt2:
                pool.wait_ge(pre_stats, NPRE * nxt2.v + 4)
                need(pool, xn_ok, 2 * (nxt2.v - 2) + 2)
                pool_rstd(pre_mv[:, nxt2.par], pre_r[:, nxt2.par], pre_rstd, 2 * nxt2.v)
            if ie:
                pool_select(ie, ge, 1)
            if k == 0 and nxt:
                pool_rest(nxt)
            if k == 1 and nxt:
                pool_part(nxt)
            if k == 0 and oldest and oldest.phase > 0:
                pool.wait_ge(hT_sb, oldest.v - B + 1)
                nc.gpsimd.tensor_copy(hT_all[:, bass.ds(oldest.b * T, T)], hT[:, oldest.par]).then_inc(hT_kept, 1)

        def sp_stack(i):
            sp.wait_ge(split, NSPLIT * i.v + NSPLIT)
            need(sp, sT_ps, 12 * (i.v - 2) + 12)
            alone(sp)
            qk = parts[:, i.par].rearrange("p w a t -> p (w a) t")
            for t, (a, b) in enumerate(TERM):
                sp.dma_start(stack[t * HD:(t + 1) * HD, i.par].rearrange("p h w t -> p (h w) t"),
                             qk[:, a:b + 4:b + 3 - a]).then_inc(stack_dma[i.par], 16)

        def sp_slot(step, k):
            nxt = item(step, 1)
            im, gm = group(step, k, 1)
            if im:
                sp.wait_ge(mT_sb, 4 * im.v + gm + 1)
                alone(sp)
                need(sp, sT_ps, 12 * (im.v - 2) + 3 * gm + 3)
                alone(sp)
                sp.dma_start(stack[SHIFT:P, im.par, HG * gm:HG * (gm + 1), 0],
                             mT[:, gm % 2, :]).then_inc(row_dma[gm % 2], 16)
            if k == 2 and nxt:
                sp_stack(nxt)

        block = ctx.enter_context(nc.Block())
        RUNS = [(0, 2 * B), (2 * B, 3 * B)]
        G0 = 19

        def dve_gate(layer):
            n = [G0 * layer]
            if layer == 0:
                dve.wait_ge(lg_sb, B)
                N, lg = NT, logits[:]
            else:
                N = B
                dve.wait_ge(lg_sb, 2 * B)
                spread = gtmp[:, 0, 0:B]
                nc.vector.tensor_tensor(spread, hmean[:].unsqueeze(2).to_broadcast([P, B, E]),
                                        gw_s[:, 1:2].to_broadcast([P, B, E]), ALU.mult).then_inc(gate_p, 1)
                dve.wait_ge(gate_p, 2)
                lg = logits[:, 0:B]
                nc.vector.scalar_tensor_tensor(out=lg, in0=pre_bank[:, 0:B * E].rearrange("p (b e) -> p b e", e=E),
                                               scalar=1.0 / T, in1=gb_s[:, 1:2].to_broadcast([P, B, E]),
                                               op0=ALU.mult, op1=ALU.add).then_inc(gate_p, 1)
                dve.wait_ge(gate_p, 3)

            def step(ins):
                n[0] += 1
                ins.then_inc(gate_v, 1)
                dve.wait_ge(gate_v, n[0])

            def wide(i):
                return gsm[:, i, 0:N].unsqueeze(2).to_broadcast([P, N, E])

            iota = iota_e[:].unsqueeze(1).to_broadcast([P, N, E])
            cur = lg
            for r in range(2):
                t, oh = gtmp[:, 1, 0:N], gtmp[:, 2 + r, 0:N]
                step(nc.vector.tensor_reduce(gsm[:, r, 0:N], cur, AX.X, ALU.max))
                step(nc.vector.tensor_tensor(t, cur, wide(r), ALU.is_equal))
                step(nc.vector.scalar_tensor_tensor(out=t, in0=t, scalar=-100.0, in1=iota, op0=ALU.mult,
                                                    op1=ALU.add))
                step(nc.vector.tensor_reduce(gsm[:, 2 + r, 0:N], t, AX.X, ALU.min))
                step(nc.vector.tensor_tensor(oh, t, wide(2 + r), ALU.is_equal))
                if r == 0:
                    step(nc.vector.scalar_tensor_tensor(out=gtmp[:, 4, 0:N], in0=oh, scalar=-3e38, in1=lg,
                                                        op0=ALU.mult, op1=ALU.add))
                    cur = gtmp[:, 4, 0:N]
            step(nc.vector.tensor_tensor(gsm[:, 4, 0:N], gsm[:, 1, 0:N], gsm[:, 0, 0:N], ALU.subtract))
            dve.wait_ge(gate_a, layer + 1)
            step(nc.vector.tensor_scalar(gsm[:, 6, 0:N], gsm[:, 5, 0:N], 1.0, None, ALU.add))
            step(nc.vector.reciprocal(gsm[:, 6, 0:N], gsm[:, 6, 0:N]))
            step(nc.vector.tensor_tensor(gsm[:, 5, 0:N], gsm[:, 5, 0:N], gsm[:, 6, 0:N], ALU.mult))
            if layer == 1:
                step(nc.vector.tensor_scalar(chosen[:], gsm[:, 2:4, 0:N], 100.0, None, ALU.add))
            step(nc.vector.tensor_tensor(gtmp[:, 2, 0:N], gtmp[:, 2, 0:N], wide(6), ALU.mult))
            step(nc.vector.tensor_tensor(gtmp[:, 3, 0:N], gtmp[:, 3, 0:N], wide(5), ALU.mult))
            nc.vector.tensor_tensor(cw[:, 0:N], gtmp[:, 2, 0:N], gtmp[:, 3, 0:N], ALU.add)\
              .then_inc(gate_v, G0 * (layer + 1) - n[0])
            dve.wait_ge(gate_v, G0 * (layer + 1))

        def act_gate(layer):
            act.wait_ge(gate_v, G0 * layer + 12)
            N = NT if layer == 0 else B
            nc.scalar.activation(gsm[:, 5, 0:N], gsm[:, 4, 0:N], ACT.Exp).then_inc(gate_a, 1)

        def pe_gate():
            pe.wait_ge(gate_p, 1)
            nc.tensor.matmul(pre_bank[:, 0:B * E], ones[:], gtmp[:, 0, 0:B].rearrange("p b e -> p (b e)"),
                             start=True, stop=True).then_inc(gate_p, 1)

        JOBS = (E, TOP)

        def jobs(layer, b):
            return B * E * layer + JOBS[layer] * b

        def pe_hidden(layer, b, e):
            j = jobs(layer, b) + e
            if layer == 1:
                pe.wait_ge(w1_got, j - B * E + 1)
            need(pe, gelu_done, FC * (j - 1))
            for c in range(FC):
                w = (w1_s, w1_job)[layer][:, e, c * P:(c + 1) * P]
                m = nc.tensor.matmul(bank[2 * (e % 2) + c // 2][:, (c % 2) * T:(c % 2 + 1) * T],
                                     w, hT_all[:, bass.ds(b * T, T)], start=True, stop=True)
                if c % 2:
                    m.then_inc(h_ps, 1)

        def pe_output(layer, b, e):
            j = jobs(layer, b) + e
            if layer == 1:
                pe.wait_ge(w2_got, j - B * E + 1)
            pe.wait_ge(gelu_done, FC * j + FC)
            need(pe, acc, 2 * (j - 1))
            for t in range(2):
                for c in range(FC):
                    m = nc.tensor.matmul(bank[4 + e % 2][:, t * P:(t + 1) * P],
                                         hid[:, e % 2, c, t * P:(t + 1) * P], (w2_s, w2_job)[layer][:, e, c],
                                         start=(c == 0), stop=(c == FC - 1))
            m.then_inc(y_ps, 1)

        def pe_experts(layer):
            tiles_of = (2, 1)[layer]

            def body(b, last):
                seq = b + B * layer
                for e in range(JOBS[layer]):
                    if e < JOBS[layer] - 1:
                        pe_hidden(layer, b, e + 1)
                    elif not last:
                        pe_hidden(layer, b + 1, 0)
                    if e == 0:
                        pe.wait_ge(cw_copied, seq + 1)
                        for t in range(tiles_of):
                            m = nc.tensor.transpose(bank[6][0:E, t * P:(t + 1) * P], cwt[:, t], ident[:])
                        m.then_inc(cwT_ps, 1)
                    if e == 1:
                        pe.wait_ge(cwT_sb, seq + 1)
                        need(pe, b2_add, seq)
                        for t in range(tiles_of):
                            m = nc.tensor.matmul(bank[7][:, t * P:(t + 1) * P], cwT[:, t * P:(t + 1) * P],
                                                 b2_s[:, layer], start=True, stop=True)
                        m.then_inc(b2_ps, 1)
                    pe_output(layer, b, e)

            pe.wait_ge(hT_kept, B * (layer + 1))
            pe.wait_ge(expert_ld[layer], 32)
            pe.wait_ge(gate_v, G0 * (layer + 1))
            pe_hidden(layer, 0, 0)
            body(0, False)
            with pe.Fori(1, B - 1) as b:
                body(b, False)
            body(B - 1, True)

        def act_experts(layer):
            def body(b):
                seq = b + B * layer
                for e in range(JOBS[layer]):
                    j = jobs(layer, b) + e
                    need(act, y_ps, j - 1)
                    if layer == 1:
                        act.wait_ge(w2_got, j - B * E + 1)
                    for c in range(FC):
                        if c % 2 == 0:
                            act.wait_ge(h_ps, 2 * j + c // 2 + 1)
                        bias = b1_s[:, 0, e, c:c + 1] if layer == 0 else b1_job[:, e, c:c + 1]
                        nc.scalar.activation(hid[:, e % 2, c],
                                             bank[2 * (e % 2) + c // 2][:, (c % 2) * T:(c % 2 + 1) * T],
                                             ACT.Gelu, bias=bias).then_inc(gelu_done, 1)
                    if e == 0:
                        act.wait_ge(cwT_ps, seq + 1)
                        need(act, b2_ps, seq)
                        nc.scalar.copy(cwT[:, 0:(2 - layer) * P], bank[6][0:E, 0:(2 - layer) * P])\
                          .then_inc(cwT_sb, 1)

            body(0)
            with act.Fori(1, B) as b:
                body(b)

        def dve_expert_w1(b, r):
            e = nc.vector.value_load(chosen[0:1, r, bass.ds(b, 1)], min_val=0, max_val=E - 1)
            need(dve, h_ps, 2 * jobs(1, b - 1) + 2 * r + 2 if not isinstance(b, int) or b > 0 else 0)
            alone(dve)
            nc.vector.tensor_copy(w1_job[:, r:r + 1], w1_s[:, bass.ds(e, 1)]).then_inc(w1_got, 1)
            return e

        def dve_expert_w2(b, r, e):
            need(dve, y_ps, jobs(1, b - 1) + r + 1 if not isinstance(b, int) or b > 0 else 0)
            alone(dve)
            nc.vector.tensor_copy(w2_job[:, r:r + 1], w2_s[:, bass.ds(e, 1)])
            nc.vector.tensor_copy(b1_job[:, r:r + 1], b1_s[:, 1, bass.ds(e, 1)]).then_inc(w2_got, 1)

        def dve_experts(layer):
            def body(b, last):
                seq = b + B * layer

                def weights(t):
                    at = 2 * b + t if layer == 0 else b
                    return cw[:, bass.ds(at, 1), :].rearrange("p a e -> p (a e)")

                need(dve, cwT_ps, seq)
                need(dve, acc, 2 * jobs(layer, b))
                for t in range(2 - layer):
                    m = nc.vector.tensor_copy(cwt[:, t], weights(t))
                if layer == 1:
                    for r in range(TOP):
                        m = nc.vector.tensor_copy(cwt[:, 1, r:r + 1], gsm[:, 6 - r, bass.ds(b, 1)])
                m.then_inc(cw_copied, 1)
                dve.wait_ge(cw_copied, seq + 1)
                for e in range(JOBS[layer]):
                    j = jobs(layer, b) + e
                    if layer == 1 and not last:
                        expert = dve_expert_w1(b + 1, e)
                    dve.wait_ge(y_ps, j + 1)
                    need(dve, acc, 2 * j)
                    for t in range(2):
                        f = f_all[:, bass.ds(2 * b + t, 1), :].rearrange("p a d -> p (a d)")
                        weight = cwt[:, t, e:e + 1] if layer == 0 else cwt[:, 1, e:e + 1]
                        nc.vector.scalar_tensor_tensor(out=f, in0=bank[4 + e % 2][:, t * P:(t + 1) * P],
                                                       scalar=weight, in1=f,
                                                       op0=ALU.mult, op1=ALU.add).then_inc(acc, 1)
                    if layer == 1 and not last:
                        dve_expert_w2(b + 1, e, expert)
                    if e == 1:
                        dve.wait_ge(b2_ps, seq + 1)
                        dve.wait_ge(acc, 2 * j + 2)
                        f = f_all[:, bass.ds(2 * b, 2), :]
                        y = bank[7][:, 0:(2 - layer) * P].rearrange("p (j d) -> p j d", d=P)
                        nc.vector.tensor_tensor(f, y if layer == 0 else y.to_broadcast([P, 2, P]), f,
                                                ALU.add).then_inc(b2_add, 1)
                        dve.wait_ge(b2_add, seq + 1)

            if layer == 1:
                dve.wait_ge(expert_ld[1], 32)
                for r in range(TOP):
                    dve_expert_w2(0, r, dve_expert_w1(0, r))
            body(0, False)
            with dve.Fori(1, B - 1) as b:
                body(b, False)
            body(B - 1, True)

        @block.sync
        def _(_):
            sp.dma_start(x_all[:, 0:8], x_dram[:, 0:8]).then_inc(x_first, 16)
            for t, d in ((wqk_s, w_qk), (bqk_s, b_qk), (ln1_s, ln1), (wv_s, w_v), (wo_s, w_o)):
                sp.dma_start(t[:], d).then_inc(small_ld, 16)
            sp.dma_start(x_all[:, 8:NT], x_dram[:, 8:NT]).then_inc(x_rest, 16)
            sp.wait_ge(qstack_ok, 1)
            sp.wait_ge(vconst_ok, 1)
            run_steps(sp, sp_slot, *RUNS[0])
            run_steps(sp, sp_slot, *RUNS[1])
            with sp.Fori(0, B) as b:
                sp.wait_ge(fin_x, b + 1)
                alone(sp)
                sp.dma_start(out_dram[:, bass.ds(2 * b, 2), :], x_all[:, bass.ds(2 * b, 2), :]).then_inc(out_dma, 16)
            sp.wait_ge(out_dma, 16 * B)

        @block.gpsimd
        def _(_):
            nc.gpsimd.memset(stack[:, :, :, 0], 0.0).then_inc(qstack_ok, 1)
            nc.gpsimd.memset(ident[:], 0.0).then_inc(const_ok, 1)
            nc.gpsimd.memset(maskneg[:], 0.0).then_inc(const_ok, 1)
            nc.gpsimd.memset(power[:], -0.5).then_inc(const_ok, 1)
            nc.gpsimd.iota(iota_e[:], pattern=[[1, E]], base=0, channel_multiplier=0,
                           allow_small_or_imprecise_dtypes=True).then_inc(const_ok, 1)
            pool.wait_ge(const_ok, 4)
            nc.gpsimd.affine_select(out=ident[:], in_=ident[:], compare_op=ALU.not_equal, fill=1.0, base=0,
                                    pattern=[[-1, P]], channel_multiplier=1).then_inc(const_ok, 1)
            nc.gpsimd.affine_select(out=maskneg[:], in_=maskneg[:], compare_op=ALU.is_ge, fill=MASKED, base=0,
                                    pattern=[[0, HG], [-1, P]], channel_multiplier=1).then_inc(const_ok, 1)
            pool.wait_ge(const_ok, 6)
            nc.gpsimd.tensor_copy(identb[:], ident[:]).then_inc(const_ok, 1)
            run_steps(pool, pool_slot, *RUNS[0])
            run_steps(pool, pool_slot, *RUNS[1])
            with pool.Fori(0, B - 1, 2) as n:
                for par in range(2):
                    pool.wait_ge(fin_v, 4 * (n + par) + 4)
                    pool_rstd(mv2[:, par], r2[:, par], fin_p, 2 * (n + par))

        @block.scalar
        def _(_):
            for t, d in ((bv_s, b_v), (bo_s, b_o), (gb_s, gate_b)):
                act.dma_start(t[:], d.partition_broadcast(P)).then_inc(small_ld, 16)
            for t, d in ((ln2_s, ln2), (gw_s, gate_w), (b1_s, e_b1), (b2_s, e_b2)):
                act.dma_start(t[:], d).then_inc(small_ld, 16)
            act.wait_ge(small_ld, SMALL)

            def load_experts(l):
                act.dma_start(w1_s[:], e_w1[l].rearrange("e d f -> d e f")).then_inc(expert_ld[l], 16)
                act.dma_start(w2_s[:].rearrange("p e c d -> p (e c) d"),
                              e_w2[l].rearrange("e (c p) d -> p (e c) d", p=P)).then_inc(expert_ld[l], 16)

            load_experts(0)
            run_steps(act, act_slot, *RUNS[0])
            act_gate(0)
            act_experts(0)
            act.wait_ge(y_ps, B * E)
            load_experts(1)
            run_steps(act, act_slot, *RUNS[1])
            act_gate(1)
            act_experts(1)

        @block.vector
        def _(_):
            nc.vector.memset(stack[:, :, :, 1], 1.0).then_inc(vconst_ok, 1)
            nc.vector.memset(vaug[:], 0.0).then_inc(vconst_ok, 1)
            dve.wait_ge(vconst_ok, 2)
            nc.vector.memset(vaug[:, :, :, :, HD:HD + 1], 1.0).then_inc(vconst_ok, 1)
            nc.vector.memset(ones[:], 1.0).then_inc(vconst_ok, 1)
            dve.wait_ge(small_ld, SMALL)
            run_steps(dve, dve_slot, *RUNS[0])
            dve_gate(0)
            dve_experts(0)
            run_steps(dve, dve_slot, *RUNS[1])
            dve_gate(1)
            dve_experts(1)
            dve.wait_ge(b2_add, 2 * B)
            def final(n):
                for par in range(2):
                    i = Item(n + par, par, 0)
                    dve_stats(tiles(f_all, i), st2, fin_v, 4 * i.v)
                    dve_moments(st2, mv2[:, par], fin_v, 4 * i.v)
                for par in range(2):
                    i = Item(n + par, par, 0)
                    dve.wait_ge(fin_p, 2 * i.v + 2)
                    dve_normal([hn[:, par, j] for j in range(2)], tiles(f_all, i), mv2[:, par], r2[:, par], fin_n)
                    dve.wait_ge(fin_n, 2 * i.v + 2)
                    nc.vector.tensor_tensor(pair(x_all, i), pair(x_all, i), hn[:, par], ALU.add).then_inc(fin_x, 1)

            with dve.Fori(0, B - 1, 2) as n:
                final(n)

        @block.tensor
        def _(_):
            pe.wait_ge(const_ok, 7)
            pe.wait_ge(vconst_ok, 4)
            pe.wait_ge(small_ld, SMALL)
            run_steps(pe, pe_slot, *RUNS[0])
            pe_experts(0)
            run_steps(pe, pe_slot, *RUNS[1])
            pe_gate()
            pe_experts(1)



def kernel(**inputs):
    import concourse.bacc as bacc
    from concourse.bass_utils import run_bass_kernel_spmd

    a = {k: np.ascontiguousarray(v) for k, v in inputs.items()}
    f = {k[7:]: v for k, v in a.items() if k.startswith("L0_ffn_")}
    x, w_qkv, w_out = a["L0_attn_x"], a["L0_attn_w_qkv"], a["L0_attn_w_out"]
    zero, one = np.zeros(P, x.dtype), np.ones(P, x.dtype)

    def by_feature(w):
        return w.reshape(-1, H, HD).transpose(0, 2, 1).reshape(w.shape)

    def rows(vectors):
        return np.stack(vectors)

    def columns(vectors):
        return np.stack(vectors, axis=-1)

    qs = [w_qkv[:, 0:P], f["wq"][0], f["wq"][1]]
    ks = [w_qkv[:, P:2 * P], f["wk"][0], f["wk"][1]]
    vs = [w_qkv[:, 2 * P:], f["wv"][0], f["wv"][1]]
    os_ = [w_out, f["wo"][0], f["wo"][1]]
    arrays = {
        "x": x,
        "w_qk": np.stack([np.stack([by_feature(q), by_feature(k)], 1) for q, k in zip(qs, ks)], 1),
        "w_v": np.stack(vs, 1),
        "w_o": np.stack(os_, 1),
        "b_qk": np.stack([columns([by_feature(q[None])[0], by_feature(k[None])[0]])
                          for q, k in zip([zero, *f["bq"]], [zero, *f["bk"]])], 1),
        "b_v": rows([zero, *f["bv"]]),
        "b_o": rows([a["L0_attn_b_out"], *f["bo"]]),
        "ln1": np.stack([columns([w, b]) for w, b in zip([one, *f["ln1_w"]], [zero, *f["ln1_b"]])], 1),
        "ln2": np.stack([columns([w, b]) for w, b in zip(f["ln2_w"], f["ln2_b"])], 1),
        "gate_w": f["gate_w"].transpose(1, 0, 2),
        "gate_b": f["gate_b"],
        "e_w1": f["e_w1"],
        "e_b1": f["e_b1"].reshape(2, E, -1, P).transpose(3, 0, 1, 2),
        "e_w2": f["e_w2"],
        "e_b2": f["e_b2"].transpose(1, 0, 2),
    }
    arrays = {k: np.ascontiguousarray(v) for k, v in arrays.items()}
    nc = bacc.Bacc("TRN2", target_bir_lowering=False, num_devices=1)
    args = [nc.dram_tensor(k, v.shape, mybir.dt.from_np(v.dtype), kind="ExternalInput").ap()
            for k, v in arrays.items()]
    out = nc.dram_tensor("out", x.shape, F32, kind="ExternalOutput").ap()
    build(nc, *args, out)
    r = run_bass_kernel_spmd(nc, [arrays], core_ids=[0])
    return r.results[0]["out"]
```

```python
from contextlib import ExitStack

import numpy as np

import concourse.bass as bass
from concourse import mybir

ALU = mybir.AluOpType
ACT = mybir.ActivationFunctionType
AX = mybir.AxisListType
F32 = mybir.dt.float32
BF16 = mybir.dt.bfloat16
I32 = mybir.dt.int32
U32 = mybir.dt.uint32

P = 128
H = 16
HD = P // H
HG = 4
NG = H // HG
E = 8
TOP = 2
EPS = 1e-5
SCALE = float(HD) ** -0.5
TWO_ONES = float(np.array([0x3F803F80], np.uint32).view(np.float32)[0])
MASKED = -1e30
TERM = [(0, 0), (0, 1), (0, 2), (1, 0), (1, 1), (2, 0)]
TERMS = len(TERM)
ROWS = TERMS * HD
SHIFT = P - 2
NPRE, NRSTD, NRES, NSPLIT = 4, 4, 14, 3
STACK_DMAS = TERMS
NTOP, NPLACE = 6, 7


def need(eng, sem, value):
    if isinstance(value, int) and value <= 0:
        return
    eng.wait_ge(sem, value)


def build(nc, x_in, w_qk, w_v, w_o, b_qk, b_v, b_o, ln1, ln2, gate_w, gate_b, e_w1, e_b1, e_w2, e_b2, out):
    B, T, D = x_in.shape
    assert D == P and T == 2 * P and B % 2 == 0 and B >= 10
    L, _, _, DFF = e_w1.shape
    FC = DFF // P
    NT = B * 2
    MAXJ = B
    JOBS = TOP * B + E
    REG = (MAXJ + 1) * T

    pe, act, dve, pool, sp = nc.tensor, nc.scalar, nc.vector, nc.gpsimd, nc.sync

    with ExitStack() as ctx:
        def sb(name, shape, dt=F32):
            return ctx.enter_context(nc.sbuf_tensor(name, shape, dt))

        def sem(name):
            return ctx.enter_context(nc.semaphore(name))

        bank = [ctx.enter_context(nc.psum_tensor(f"bank{i}", [P, 512], F32)) for i in range(8)]
        max_bank, exp_bank = bank[0:2], bank[2:4]
        pv_bank, pre_bank, mid_bank, post_bank = bank[4:8]
        v_bank, lg_bank = post_bank[:, 0:T], post_bank[:, T:T + 2 * E]
        rank_bank, sum_bank = post_bank[:, T + 4 * E:T + 6 * E], post_bank[:, T + 6 * E:T + 7 * E]

        x_all = sb("x_all", [P, NT, P])
        f_all = sb("f_all", [P, NT, P])
        hT_all = sb("hT_all", [P, NT * P])
        wqk_s = sb("wqk_s", [P, 3, 2, P])
        wv_s = sb("wv_s", [P, 3, P])
        wo_s = sb("wo_s", [P, 3, P])
        bqk_s = sb("bqk_s", [P, 3, 2])
        bv_s = sb("bv_s", [P, 3, P])
        bo_s = sb("bo_s", [P, 3, P])
        ln1_s = sb("ln1_s", [P, 3, 2])
        ln2_s = sb("ln2_s", [P, L, 2])
        gw_s = sb("gw_s", [P, L, E])
        gb_s = sb("gb_s", [P, L, E])
        w1_s = sb("w1_s", [P, E, DFF])
        w2_s = sb("w2_s", [P, E, FC, P])
        b1_s = sb("b1_s", [P, L, E, FC])
        ident = sb("ident", [P, P])
        identb = sb("identb", [P, P], BF16)
        maskneg = sb("maskneg", [P, HG, P], BF16)
        ones = sb("ones", [P, P])
        power = sb("power", [P, 2])
        iota_e = sb("iota_e", [P, E])
        pre_st = sb("pre_st", [P, 2, 6])
        pre_mv = sb("pre_mv", [P, 2, 2, 2])
        pre_r = sb("pre_r", [P, 2, 2])
        xn = sb("xn", [P, 2, 2, P])
        xT = sb("xT", [P, 2, T])
        qkf = sb("qkf", [P, 2, T])
        rest = sb("rest", [P, 2, T])
        parts = sb("parts", [P, 2, 2, 3, T], BF16)
        stack = sb("stack", [P, 2, H, 2, T], BF16)
        vaug = sb("vaug", [P, 2, 2, H, 32])
        negm = sb("negm", [P, 2, 2, HG])
        mparts = sb("mparts", [P, 2, 2, 2, HG], BF16)
        mT = sb("mT", [2 * HG, 2, T], BF16)
        prob1 = sb("prob1", [P, 2, HG, P])
        prob0 = sb("prob0", [P, 2, HG, T])
        oT = sb("oT", [P, 2, NG, T])
        rden = sb("rden", [P, 2, H])
        on = sb("on", [P, 2, 2, P])
        onT = sb("onT", [P, 2, T])
        att = sb("att", [P, 2, 2, P])
        post_st = sb("post_st", [P, 2, 6])
        post_mv = sb("post_mv", [P, 2, 2, 2])
        post_r = sb("post_r", [P, 2, 2])
        st2 = sb("st2", [P, 2, 6])
        mv2 = sb("mv2", [P, 2, 2, 2])
        r2 = sb("r2", [P, 2, 2])
        hn = sb("hn", [P, 2, 2, P])
        hT = sb("hT", [P, 2, T])
        logits = sb("logits", [P, B, E])
        hmean = sb("hmean", [P, B])
        gtmp = sb("gtmp", [P, 4, B, E])
        gsm = sb("gsm", [P, 7, B])
        hid = prob0
        chosen = sb("chosen", [P, TOP, B], I32)
        w1_job = sb("w1_job", [P, TOP, DFF])
        w2_job = sb("w2_job", [P, TOP, FC, P])
        b1_job = sb("b1_job", [P, TOP, FC])
        b2_all = sb("b2_all", [P, E, P])
        onesb = sb("onesb", [P, P], BF16)
        before = sb("before", [P, P], BF16)
        lgt = sb("lgt", [P, 2, E])
        mx = sb("mx", [P, 2, 8])
        mi = sb("mi", [P, 2, 8], U32)
        gap_all = sb("gap_all", [P, NT])
        expert_all = sb("expert_all", [P, NT, TOP])
        place_all = sb("place_all", [P, NT, TOP])
        weight_all = sb("weight_all", [P, NT, TOP])
        onehot = sb("onehot", [P, 2, TOP, E])
        either = sb("either", [P, 2, E], BF16)
        places = sb("places", [P, 2, E])
        picked = sb("picked", [P, 2, TOP, E])
        counts = sb("counts", [P, E])
        x_at = sb("x_at", [P, 2, 2, TOP], U32)
        hk = sb("hk", [P, 2, 2, P])
        iota_j = sb("iota_j", [P, JOBS])
        earlier = sb("earlier", [P, E, E])
        tb = prob1[:, 0].rearrange("p h q -> p (h q)")
        assert max(JOBS * E, NT * TOP * E) <= HG * P
        nj, js = sb("nj", [P, E]), sb("js", [P, E])
        total = sb("total", [P, 1])
        jt = sb("jt", [P, 5, JOBS])
        job_e, job_row = sb("job_e", [P, JOBS], I32), sb("job_row", [P, JOBS], I32)
        pad_row = sb("pad_row", [P, E], I32)
        y_at_all = sb("y_at_all", [P, NT, TOP], U32)
        zeros = sb("zeros", [P, 2, P])
        xj = oT[:, 0, 0:2].rearrange("p i (t d) -> p i t d", t=2)
        xjT = oT[:, 0, 2:4]
        yj = oT[:, 1, 0:2].rearrange("p i (t d) -> p i t d", t=2)
        b2_job = oT[:, 1, 2].rearrange("p (i d) -> p i d", i=2)
        y_at = sb("y_at", [P, 2, 2, TOP], U32)
        y_got = sb("y_got", [P, 2, 2, TOP, P])
        x_routed = nc.dram_tensor("x_routed", [E * REG + T, P], F32, kind="Internal").ap()
        y_routed = nc.dram_tensor("y_routed", [JOBS * T, P], F32, kind="Internal").ap()

        const_ok, waited = sem("const_ok"), sem("waited")
        vconst_ok, qstack_ok, kstack_ok = sem("vconst_ok"), sem("qstack_ok"), sem("kstack_ok")
        x_first, x_rest = sem("x_first"), sem("x_rest")
        small_ld, later_ld = sem("small_ld"), sem("later_ld")
        expert_ld = [sem("expert_ld0"), sem("expert_ld1")]
        pre_stats, pre_rstd, xn_ok = sem("pre_stats"), sem("pre_rstd"), sem("xn_ok")
        xT_ps, xT_sb, qk_ps, v_ps = sem("xT_ps"), sem("xT_sb"), sem("qk_ps"), sem("v_ps")
        qkf_sb, split, v_sb = sem("qkf_sb"), sem("split"), sem("v_sb")
        stack_dma = [sem("stack_dma0"), sem("stack_dma1")]
        row_dma = [sem("row_dma0"), sem("row_dma1")]
        max_ps, max_done, negmax = sem("max_ps"), sem("max_done"), sem("negmax")
        maxT_ps, mT_sb = sem("maxT_ps"), sem("mT_sb")
        sT_ps, exp_done, sel_done, pv_ps, ot_sb = sem("sT_ps"), sem("exp_done"), sem("sel_done"), sem("pv_ps"), sem("ot_sb")
        o1_ps, attn_n, o2_ps, onT_sb, o3_ps = sem("o1_ps"), sem("attn_n"), sem("o2_ps"), sem("onT_sb"), sem("o3_ps")
        res, post_rstd = sem("res"), sem("post_rstd")
        hT_ps, hT_sb, lg_ps, lg_sb = sem("hT_ps"), sem("hT_sb"), sem("lg_ps"), sem("lg_sb")
        gate_v, gate_a, gate_p = sem("gate_v"), sem("gate_a"), sem("gate_p")
        h_ps, gelu_done, y_ps, acc = sem("h_ps"), sem("gelu_done"), sem("y_ps"), sem("acc")
        w1_got, b1_got, w2_got = sem("w1_got"), sem("b1_got"), sem("w2_got")
        top, placed, rank_ps, hk_sb = sem("top"), sem("placed"), sem("rank_ps"), sem("hk_sb")
        x_sent = [sem("x_sent0"), sem("x_sent1")]
        table, pad_dma, zeros_dma = sem("table"), sem("pad_dma"), sem("zeros_dma")
        x_got = [sem("x_got0"), sem("x_got1")]
        y_sent = [sem("y_sent0"), sem("y_sent1")]
        xjT_ps, xjT_sb, yj_sb = sem("xjT_ps"), sem("xjT_sb"), sem("yj_sb")
        fetch_at, combined = sem("fetch_at"), sem("combined")
        y_fetch = [sem("y_fetch0"), sem("y_fetch1")]
        bias_ld, bias_add = sem("bias_ld"), sem("bias_add")
        fin_v, fin_q, fin_p, fin_n, fin_x, out_dma = sem("fin_v"), sem("fin_q"), sem("fin_p"), sem("fin_n"), sem("fin_x"), sem("out_dma")

        SMALL, LATER = 5 * 16, 7 * 16
        x_dram = x_in.rearrange("b (j p) d -> p (b j) d", p=P)
        out_dram = out.rearrange("b (j p) d -> p (b j) d", p=P)

        class Item:
            def __init__(self, v, par, phase):
                self.v, self.par, self.phase = v, par, phase
                self.b = v - phase * B

        def item(step, d):
            n, par, phase, lo, hi = step
            if isinstance(n, int):
                v = n + d
                return Item(v, v % 2, v // B) if lo <= v < hi else None
            return Item(n + d, (par + d) % 2, phase)

        def step_phase(step):
            n, par, phase, lo, hi = step
            return 2 if lo == 2 * B else 1

        def group(step, k, lag):
            d, g = divmod(k - lag, NG)
            return item(step, d), g

        def run_steps(eng, slot, lo, hi):
            def peeled(a, b):
                for n in range(a, b):
                    for k in range(NG):
                        slot((n, n % 2, None, lo, hi), k)

            at = lo - (3 if hi == 3 * B else 2)
            for phase in range(lo // B, hi // B):
                first, last = phase * B + (6 if phase == 1 else 4), phase * B + B - (4 if phase == 2 else 2)
                peeled(at, first)
                with eng.Fori(first, last - 1, 2) as n:
                    for d in range(2):
                        for k in range(NG):
                            slot((n + d, d, phase, lo, hi), k)
                at = last
            peeled(at, hi + (6 if hi == 2 * B else 3))

        def behind(slot, step, then):
            def both(at, k):
                slot(at, k)
                n = (at[0] - step) * NG + k if isinstance(at[0], int) else -1
                if 0 <= n < len(then):
                    then[n]()
            return both

        def alone(eng):
            eng.sem_inc(waited, 1)

        def unit(i, g, u):
            return 12 * i.v + 3 * g + u + 1

        def stack_ready(i):
            return 8 * STACK_DMAS * (i.v + (2 if i.par == 0 else 1))

        def rows_ready(i, g):
            return 32 * i.v + 16 * (g // 2 + 1)

        def pe_max(i, g, u):
            p0 = HG * g
            if g == 0 and u == 0:
                pe.wait_ge(stack_dma[i.par], stack_ready(i))
            need(pe, max_done, unit(i, g, u) - 2)
            bk = max_bank[(g + u) % 2]
            q, k = stack[0:SHIFT, i.par, :, 0], stack[0:SHIFT, i.par, :, 1]
            if u == 0:
                o = bk[:].rearrange("p (h k) -> p h k", h=HG)
                nc.tensor.matmul(o, identb[:], maskneg[:], start=True, stop=False, skip_group_check=True)
                for h in range(HG):
                    m = nc.tensor.matmul(o[:, h], q[:, p0 + h, 0:P], k[:, p0 + h, 0:P],
                                         start=False, stop=True, skip_group_check=True)
            else:
                o = bk[:].rearrange("p (h k) -> p h k", h=2)
                nc.tensor.matmul(o[:, :, P:T], identb[:], maskneg[:, 0:2], start=True, stop=False,
                                 skip_group_check=True)
                for h in range(2):
                    hh = p0 + 2 * (u - 1) + h
                    m = nc.tensor.matmul(o[:, h], q[:, hh, P:T], k[:, hh, :],
                                         start=False, stop=True, skip_group_check=True)
            m.then_inc(max_ps, 1)

        def pe_scores(i, g, u):
            p0 = HG * g
            if u == 0:
                pe.wait_ge(row_dma[g % 2], rows_ready(i, g))
            need(pe, exp_done, unit(i, g, u) - 2)
            bk = exp_bank[(g + u) % 2]
            q, k = stack[:, i.par, :, 0], stack[:, i.par, :, 1]
            if u == 0:
                for h in range(HG):
                    m = nc.tensor.matmul(bk[:, h * P:(h + 1) * P], k[:, p0 + h, P:T], q[:, p0 + h, P:T],
                                         start=True, stop=True)
            else:
                for h in range(2):
                    hh = p0 + 2 * (u - 1) + h
                    m = nc.tensor.matmul(bk[:, h * T:(h + 1) * T], k[:, hh, 0:P], q[:, hh, :],
                                         start=True, stop=True)
            m.then_inc(sT_ps, 1)

        def pe_values(i, g, half):
            G = 4 * i.v + g
            if half == 0:
                need(pe, v_sb, i.v + 1)
                pe.wait_ge(sel_done, 2 * G + 2)
                need(pe, ot_sb, G)
            for h in range(2 * half, 2 * half + 2):
                head = HG * g + h
                o = pv_bank[32 * h:32 * h + 32, 0:T]
                nc.tensor.matmul(o, vaug[:, i.par, 0, head], prob0[:, g % 2, h], start=True, stop=False,
                                 skip_group_check=True)
                m = nc.tensor.matmul(o[:, P:T], vaug[:, i.par, 1, head], prob1[:, g % 2, h],
                                     start=False, stop=True, skip_group_check=True)
            if half == 1:
                m.then_inc(pv_ps, 1)

        def pe_max_T(i, g):
            G = 4 * i.v + g
            pe.wait_ge(negmax, 2 * G + 2)
            need(pe, mT_sb, G)
            o = mid_bank[0:2 * HG, 0:P].bitcast(BF16)
            for qb in range(2):
                m = nc.tensor.transpose(o[:, qb * P:(qb + 1) * P],
                                        mparts[:, g % 2, qb].rearrange("p a h -> p (a h)"), identb[:])
            m.then_inc(maxT_ps, 1)

        def pe_xT(i):
            pe.wait_ge(xn_ok, 2 * i.v + 2)
            need(pe, qkf_sb, 4 * i.v)
            for j in range(2):
                m = nc.tensor.transpose(pre_bank[:, j * P:(j + 1) * P], xn[:, i.par, j], ident[:])
            m.then_inc(xT_ps, 1)

        def pe_qk(i):
            pe.wait_ge(xT_sb, i.v + 1)
            if i.v - 4 >= B if isinstance(i.v, int) else i.phase > 0:
                pe.wait_ge(hT_sb, i.v - 4 - B + 1)
            for t in range(2):
                m = nc.tensor.matmul(pre_bank[:, t * T:(t + 1) * T], wqk_s[:, i.phase, t], xT[:, i.par],
                                     start=True, stop=True)
            m.then_inc(qk_ps, 1)

        def pe_v(i):
            for j in range(2):
                m = nc.tensor.matmul(v_bank[:, j * P:(j + 1) * P], xT[:, i.par, j * P:(j + 1) * P],
                                     wv_s[:, i.phase], start=True, stop=True)
            m.then_inc(v_ps, 1)

        def pe_o1(i, qb):
            if qb == 0:
                pe.wait_ge(ot_sb, 4 * i.v + 4)
                need(pe, res, NRES * (i.v - 1) + 1)
            else:
                pe.wait_ge(attn_n, 4 * i.v + 2)
            for g in range(NG):
                m = nc.tensor.transpose(post_bank[:, g * P:(g + 1) * P], oT[:, i.par, g, qb * P:(qb + 1) * P],
                                        ident[:])
            m.then_inc(o1_ps, 1)

        def pe_o2(i):
            pe.wait_ge(attn_n, 4 * i.v + 4)
            for qb in range(2):
                m = nc.tensor.transpose(post_bank[:, qb * P:(qb + 1) * P], on[:, i.par, qb], ident[:])
            m.then_inc(o2_ps, 1)

        def pe_o3(i):
            pe.wait_ge(onT_sb, i.v + 1)
            for qb in range(2):
                m = nc.tensor.matmul(post_bank[:, qb * P:(qb + 1) * P], onT[:, i.par, qb * P:(qb + 1) * P],
                                     wo_s[:, i.phase], start=True, stop=True)
            m.then_inc(o3_ps, 1)

        def pe_hT(i):
            pe.wait_ge(res, NRES * i.v + NRES)
            end = (2 if i.v < 2 * B else 3) * B if isinstance(i.v, int) else None
            pe.wait_ge(qkf_sb, 4 * (min(i.v + 4, end) if end else i.v + 4))
            for j in range(2):
                m = nc.tensor.transpose(pre_bank[:, T + j * P:T + (j + 1) * P], hn[:, i.par, j], ident[:])
            m.then_inc(hT_ps, 1)

        def pe_logits(i):
            pe.wait_ge(hT_sb, i.v - B + 1)
            need(pe, lg_sb, i.v - B)
            for j in range(2):
                m = nc.tensor.matmul(lg_bank[:, j * E:(j + 1) * E], hT[:, i.par, j * P:(j + 1) * P],
                                     gw_s[:, 0], start=True, stop=True)
            m.then_inc(lg_ps, 1)

        def pe_rank(i):
            u = i.v - B
            pe.wait_ge(placed, NPLACE * u + 2)
            a = either[:].rearrange("p t e -> p (t e)")
            nc.tensor.matmul(rank_bank, before[:], a, start=True, stop=False, skip_group_check=True)
            nc.tensor.matmul(rank_bank[:, E:2 * E], onesb[:], either[:, 0], start=False, stop=True,
                             skip_group_check=True)
            nc.tensor.matmul(sum_bank, onesb[:], either[:, 0], start=True, stop=False, skip_group_check=True)
            nc.tensor.matmul(sum_bank, onesb[:], either[:, 1], start=False, stop=True,
                             skip_group_check=True).then_inc(rank_ps, 1)

        def pe_slot(step, k):
            first = item(step, -4)
            cur, nxt, nxt2, old, older, oldest = (item(step, d) for d in (0, 1, 2, -1, -2, -3))
            (ie, ge), (iv, gv), (im, gm) = group(step, k, 2), group(step, k, 3), group(step, k, 1)
            if cur:
                pe_max(cur, k, 0)
            if ie:
                pe_scores(ie, ge, 0)
            if k == 0 and nxt:
                pe_qk(nxt)
            if k == 3 and old:
                if nxt:
                    pe.wait_ge(v_sb, nxt.v + 1)
                if oldest and oldest.phase == 1:
                    pe.wait_ge(lg_sb, oldest.v - B + 1)
                if first and first.phase == 1:
                    pe.wait_ge(placed, NPLACE * (first.v - B) + 4)
                pe_o1(old, 0)
            if im:
                pe_max_T(im, gm)
            if cur:
                pe_max(cur, k, 1)
            if ie:
                pe_scores(ie, ge, 1)
            if iv:
                pe_values(iv, gv, 0)
            if k == 0 and older:
                pe_o2(older)
            if k == 3 and older and older.phase > 0:
                pe_hT(older)
            if cur:
                pe_max(cur, k, 2)
            if ie:
                pe_scores(ie, ge, 2)
            if iv:
                pe_values(iv, gv, 1)
            if k == 0 and older:
                pe_o3(older)
            if k == 1 and older and (nxt or oldest and oldest.phase == 1):
                pe.wait_ge(res, NRES * older.v + 1)
            if k == 1 and oldest and oldest.phase == 1:
                pe_logits(oldest)
            if k == 1 and first and first.phase == 1:
                pe_rank(first)
            if k == 1 and nxt:
                pe_v(nxt)
            if k == 3 and older and older.phase > 0 and nxt2:
                pe.wait_ge(hT_sb, older.v - B + 1)
            if k == 3 and nxt2:
                pe_xT(nxt2)
            if k == 3 and old:
                pe_o1(old, 1)

        def act_exp(i, g, u):
            act.wait_ge(sT_ps, unit(i, g, u))
            if u == 0:
                need(act, pv_ps, 4 * i.v + g - 1)
            bk = exp_bank[(g + u) % 2]
            if u == 0:
                o, s = prob1[:, g % 2].rearrange("p h q -> p (h q)"), bk[:]
            else:
                o, s = prob0[:, g % 2, 2 * u - 2:2 * u].rearrange("p h q -> p (h q)"), bk[:]
            nc.scalar.activation(o, s, ACT.Exp, scale=SCALE).then_inc(exp_done, 1)

        def act_oT(i, g):
            act.wait_ge(pv_ps, 4 * i.v + g + 1)
            if g == 0:
                need(act, o1_ps, 2 * (i.v - 2) + 2)
            nc.scalar.copy(oT[:, i.par, g], pv_bank[:, 0:T]).then_inc(ot_sb, 1)

        def act_qk(i, t):
            if t == 0:
                act.wait_ge(qk_ps, i.v + 1)
                need(act, split, NSPLIT * (i.v - 1) + 1)
                need(act, stack_dma[i.par], stack_ready(i) - 16 * STACK_DMAS)
            for o in (qkf[:, t], parts[:, i.par, t, 0]):
                nc.scalar.activation(o, pre_bank[:, t * T:(t + 1) * T], ACT.Identity,
                                     bias=bqk_s[:, i.phase, t:t + 1]).then_inc(qkf_sb, 1)

        def act_part(i):
            act.wait_ge(split, NSPLIT * i.v + 1)
            nc.scalar.copy(parts[:, i.par, :, 1], rest[:]).then_inc(split, 1)

        def act_slot(step, k):
            cur, nxt, nxt2, old, older = (item(step, d) for d in (0, 1, 2, -1, -2))
            (ie, ge), (io, go) = group(step, k, 2), group(step, k, 4)
            if io:
                act_oT(io, go)
            if ie:
                act_exp(ie, ge, 0)
            if k == 0 and nxt:
                act_qk(nxt, 0)
            if ie:
                act_exp(ie, ge, 1)
            if k == 1 and nxt:
                act_part(nxt)
            if k == 0 and older:
                act.wait_ge(o2_ps, older.v + 1)
                need(act, o3_ps, older.v - 1)
                nc.scalar.copy(onT[:, older.par], post_bank[:, 0:T]).then_inc(onT_sb, 1)
            if k == 3 and older and older.phase > 0:
                act.wait_ge(hT_ps, older.v - B + 1)
                if older.phase == 1:
                    need(act, lg_ps, older.v - B - 1)
                    rows = hT[:, older.par]
                else:
                    rows = hT_all[:, bass.ds(older.b * T, T)]
                nc.scalar.activation(rows, pre_bank[:, T:2 * T], ACT.Identity,
                                     scale=ln2_s[:, older.phase - 1, 0:1], bias=ln2_s[:, older.phase - 1, 1:2])\
                  .then_inc(hT_sb, 1)
            if ie:
                act_exp(ie, ge, 2)
            if k == 0 and nxt:
                act_qk(nxt, 1)
            if k == 3 and nxt2:
                act.wait_ge(xT_ps, nxt2.v + 1)
                need(act, v_ps, nxt2.v - 1)
                nc.scalar.activation(xT[:, nxt2.par], pre_bank[:, 0:T], ACT.Identity,
                                     scale=ln1_s[:, nxt2.phase, 0:1], bias=ln1_s[:, nxt2.phase, 1:2])\
                  .then_inc(xT_sb, 1)

        def dve_reduce(i, g, u):
            dve.wait_ge(max_ps, unit(i, g, u))
            if u == 0:
                need(dve, negmax, 2 * (4 * i.v + g) - 2)
            bk = max_bank[(g + u) % 2]
            if u == 0:
                o, s = negm[:, g % 2, 0], bk[:].rearrange("p (h k) -> p h k", h=HG)
            else:
                o, s = negm[:, g % 2, 1, 2 * u - 2:2 * u], bk[:].rearrange("p (h k) -> p h k", h=2)
            nc.vector.tensor_reduce(o, s, AX.X, ALU.max, negate=True).then_inc(max_done, 1)

        def dve_split_max(i, g):
            G = 4 * i.v + g
            dve.wait_ge(max_done, unit(i, g, 2))
            need(dve, maxT_ps, G - 1)
            nc.vector.tensor_copy(mparts[:, g % 2, :, 0], negm[:, g % 2]).then_inc(negmax, 1)
            dve.wait_ge(negmax, 2 * G + 1)
            nc.vector.tensor_tensor(mparts[:, g % 2, :, 1], negm[:, g % 2], mparts[:, g % 2, :, 0],
                                    ALU.subtract).then_inc(negmax, 1)

        def dve_mT(i, g):
            dve.wait_ge(maxT_ps, 4 * i.v + g + 1)
            need(dve, row_dma[g % 2], rows_ready(i, g) - 16)
            nc.vector.tensor_copy(mT[:, g % 2], mid_bank[0:2 * HG, 0:P].bitcast(BF16)).then_inc(mT_sb, 1)

        def dve_norm(i, qb):
            dve.wait_ge(o1_ps, 2 * i.v + qb + 1)
            o = post_bank[:].rearrange("p (h c) -> p h c", c=32)
            need(dve, o2_ps, i.v - 1)
            nc.vector.reciprocal(rden[:, qb], o[:, :, HD]).then_inc(attn_n, 1)
            dve.wait_ge(attn_n, 4 * i.v + 2 * qb + 1)
            nc.vector.tensor_tensor(on[:, i.par, qb].rearrange("p (h d) -> p h d", d=HD), o[:, :, 0:HD],
                                    rden[:, qb].unsqueeze(2).to_broadcast([P, H, HD]),
                                    ALU.mult).then_inc(attn_n, 1)

        def dve_stats(src, st, s, base):
            need(dve, s, base)
            alone(dve)
            for j in range(2):
                nc.vector.bn_stats(st[:, j], src[j]).then_inc(s, 1)

        def dve_moments(st, mv, s, base):
            dve.wait_ge(s, base + 2)
            alone(dve)
            for j in range(2):
                nc.vector.bn_aggr(mv[:, j], st[:, j]).then_inc(s, 1)

        def tiles(t, i):
            return [t[:, bass.ds(2 * i.b + j, 1), :].rearrange("p a d -> p (a d)") for j in range(2)]

        def pair(t, i):
            return t[:, bass.ds(2 * i.b, 2), :]

        def dve_normal(dst, src, mv, r, s, last=1):
            for j in range(2):
                nc.vector.tensor_scalar(dst[j], src[j], mv[:, j, 0:1], r[:, j:j + 1],
                                        ALU.subtract, ALU.mult).then_inc(s, last if j else 1)

        def dve_residual(i):
            base = NRES * i.v
            dve.wait_ge(o3_ps, i.v + 1)
            nc.vector.tensor_tensor(att[:, i.par], post_bank[:, 0:T].rearrange("p (j d) -> p j d", j=2),
                                    bo_s[:, i.phase:i.phase + 1].to_broadcast([P, 2, P]),
                                    ALU.add).then_inc(res, 1)
            if i.phase > 0:
                dve.wait_ge(res, base + 1)
                nc.vector.tensor_tensor(pair(f_all, i), pair(f_all, i), att[:, i.par], ALU.add).then_inc(res, 1)

        def summed(i):
            return NRES * i.v + (2 if i.phase > 0 else 1)

        def dve_residual_stats(i):
            src = tiles(f_all, i) if i.phase > 0 else [att[:, i.par, j] for j in range(2)]
            dve_stats(src, post_st, res, summed(i))

        def dve_residual_moments(i):
            need(dve, post_rstd, NRSTD * (i.v - 2) + 2)
            dve_moments(post_st, post_mv[:, i.par], res, summed(i))

        def dve_normalise(i):
            dve.wait_ge(post_rstd, NRSTD * i.v + (2 if i.phase == 0 else NRSTD))
            if i.phase > 0:
                need(dve, hT_ps, i.v - B - 1)
                if i.phase == 1:
                    need(dve, hk_sb, i.v - B - 1)
                dve_normal([hn[:, i.par, j] for j in range(2)], tiles(f_all, i), post_mv[:, i.par],
                           post_r[:, i.par], res, NRES - 7)
            else:
                att_j = [att[:, i.par, j] for j in range(2)]
                dve_normal(att_j, att_j, post_mv[:, i.par], post_r[:, i.par], res)

        def dve_x(i):
            dve.wait_ge(res, NRES * i.v + 7)
            nc.vector.tensor_tensor(pair(x_all, i), pair(x_all, i), att[:, i.par], ALU.add).then_inc(res, 1)

        def dve_f(i):
            dve.wait_ge(post_rstd, NRSTD * i.v + NRSTD)
            dve_normal(tiles(f_all, i), tiles(x_all, i), mv2[:, i.par], r2[:, i.par], res)

        def dve_values(i):
            dve.wait_ge(v_ps, i.v + 1)
            need(dve, pv_ps, 4 * (i.v - 2) + 4)
            for j in range(2):
                m = nc.vector.tensor_tensor(vaug[:, i.par, j, :, 0:HD],
                                            v_bank[:, j * P:(j + 1) * P].rearrange("p (h d) -> p h d", h=H),
                                            bv_s[:, i.phase].rearrange("p (h d) -> p h d", h=H), ALU.add)
            m.then_inc(v_sb, 1)

        def dve_logits(i):
            dve.wait_ge(lg_ps, i.v - B + 1)
            need(dve, top, NTOP * (i.v - B))
            nc.vector.tensor_tensor(lgt[:], lg_bank.rearrange("p (j e) -> p j e", j=2),
                                    gb_s[:, 0:1].to_broadcast([P, 2, E]), ALU.add).then_inc(lg_sb, 1)

        def dve_top(i, piece):
            u = i.v - B
            at = NTOP * u
            if piece == 0:
                dve.wait_ge(lg_sb, u + 1)
                need(dve, top, at)
                alone(dve)
                for j in range(2):
                    nc.vector.max(out=mx[:, j], in_=lgt[:, j]).then_inc(top, 1)
            elif piece == 1:
                dve.wait_ge(top, at + 2)
                alone(dve)
                for j in range(2):
                    nc.vector.max_index(out=mi[:, j], in_max=mx[:, j], in_values=lgt[:, j]).then_inc(top, 1)
                gap = gap_all[:, bass.ds(2 * i.b, 2)]
                nc.vector.tensor_tensor(gap, mx[:, :, 1], mx[:, :, 0], ALU.subtract).then_inc(top, 1)
            else:
                dve.wait_ge(top, at + 4)
                alone(dve)
                nc.vector.tensor_copy(expert_all[:, bass.ds(2 * i.b, 2)], mi[:, :, 0:TOP]).then_inc(top, 1)

        def dve_place(i, piece):
            u = i.v - B
            at = NPLACE * u
            expert = expert_all[:, bass.ds(2 * i.b, 2)]
            place = place_all[:, bass.ds(2 * i.b, 2)]
            if piece == 0:
                dve.wait_ge(top, NTOP * u + NTOP)
                need(dve, placed, at)
                alone(dve)
                nc.vector.tensor_tensor(onehot[:].rearrange("p t r e -> p (t r) e"),
                                        expert.rearrange("p t r -> p (t r)").unsqueeze(2)
                                        .to_broadcast([P, 2 * TOP, E]),
                                        iota_e[:].unsqueeze(1).to_broadcast([P, 2 * TOP, E]),
                                        ALU.is_equal).then_inc(placed, 1)
            elif piece == 1:
                dve.wait_ge(placed, at + 1)
                need(dve, rank_ps, u)
                nc.vector.tensor_tensor(either[:], onehot[:, :, 0], onehot[:, :, 1], ALU.add).then_inc(placed, 1)
            elif piece == 2:
                dve.wait_ge(rank_ps, u + 1)
                nc.vector.tensor_tensor(places[:], rank_bank.rearrange("p (t e) -> p t e", t=2),
                                        counts[:].unsqueeze(1).to_broadcast([P, 2, E]), ALU.add)\
                  .then_inc(placed, 1)
                dve.wait_ge(placed, at + 3)
                nc.vector.tensor_tensor(counts[:], sum_bank, counts[:], ALU.add).then_inc(placed, 1)
            elif piece == 3:
                dve.wait_ge(placed, at + 4)
                for t in range(2):
                    m = nc.vector.tensor_tensor(picked[:, t], onehot[:, t],
                                                places[:, t:t + 1].to_broadcast([P, TOP, E]), ALU.mult)
                m.then_inc(placed, 1)
            elif piece == 4:
                dve.wait_ge(placed, at + 5)
                nc.vector.tensor_reduce(place, picked[:], AX.X, ALU.add).then_inc(placed, 1)
            else:
                dve.wait_ge(placed, at + 6)
                need(dve, x_sent[i.par], sent(i) - 16 * 2 * TOP)
                nc.vector.scalar_tensor_tensor(out=x_at[:, i.par], in0=expert, scalar=float(REG), in1=place,
                                               op0=ALU.mult, op1=ALU.add).then_inc(placed, 1)

        def sent(i):
            return 8 * 2 * TOP * (i.v - B + (2 if i.par == 0 else 1))

        def dve_combine(i, rank):
            u = i.v - 2 * B
            if rank == 0:
                dve.wait_ge(y_fetch[i.par], fetched(i))
            else:
                dve.wait_ge(combined, 4 * u + 2)
            for t, f in enumerate(tiles(f_all, i)):
                nc.vector.scalar_tensor_tensor(out=f, in0=y_got[:, i.par, t, rank],
                                               scalar=weight_all[:, bass.ds(2 * i.b + t, 1), rank], in1=f,
                                               op0=ALU.mult, op1=ALU.add).then_inc(combined, 1)

        def fetched(i):
            return 8 * 2 * TOP * (i.v - 2 * B + (2 if i.par == 0 else 1))

        def dve_mean(i):
            dve.wait_ge(hT_sb, i.v - B + 1)
            nc.vector.tensor_reduce(hmean[:, bass.ds(i.b, 1)], hT_all[:, bass.ds(i.b * T, T)], AX.X,
                                    ALU.add).then_inc(lg_sb, 1)

        def dve_input(i):
            if i.phase == 0:
                dve.wait_ge(*((x_first, 16) if isinstance(i.v, int) and i.v < 4 else (x_rest, 16)))
            elif i.phase == 1:
                dve.wait_ge(res, NRES * (i.v - B) + NRES)
            else:
                dve.wait_ge(combined, 4 * (i.v - 2 * B) + 4)
            return tiles(x_all if i.phase == 0 else f_all, i)

        def dve_slot(step, k):
            cur, nxt, nxt2, old, older, oldest, first = (item(step, d) for d in (0, 1, 2, -1, -2, -3, -4))
            im, gm = group(step, k, 1)
            ranked, placing = oldest and oldest.phase == 1, first and first.phase == 1
            if cur:
                dve_reduce(cur, k, 0)
            if im:
                dve_mT(im, gm)
            if k == 0 and older:
                dve_norm(older, 1)
            if k == 0 and oldest and oldest.phase == 2:
                dve_mean(oldest)
            if k == 1 and older:
                dve_residual(older)
            if k == 2 and nxt2:
                dve_stats(dve_input(nxt2), pre_st, pre_stats, NPRE * nxt2.v)
            if k == 2 and older:
                dve_residual_moments(older)
            if k == 2 and placing:
                dve_place(first, 2)
            if k == 3 and older and older.phase == 0:
                dve_x(older)
            if k == 3 and nxt2:
                dve.wait_ge(pre_rstd, 2 * nxt2.v + 2)
                need(dve, xT_ps, nxt2.v - 1)
                dve_normal([xn[:, nxt2.par, j] for j in range(2)], tiles(x_all if nxt2.phase == 0 else f_all, nxt2),
                           pre_mv[:, nxt2.par], pre_r[:, nxt2.par], xn_ok)
            if k == 3 and old:
                dve_norm(old, 0)
            if k == 3 and placing:
                dve_place(first, 3)
            if cur:
                dve_reduce(cur, k, 1)
            if k == 0 and nxt2 and nxt2.phase == 2:
                dve_combine(nxt2, 0)
            if k == 0 and oldest and oldest.phase == 0:
                dve_f(oldest)
            if k == 0 and placing:
                dve_place(first, 0)
            if k == 1 and older:
                dve_residual_stats(older)
            if k == 2 and nxt2:
                need(dve, pre_rstd, 2 * (nxt2.v - 2) + 2)
                dve_moments(pre_st, pre_mv[:, nxt2.par], pre_stats, NPRE * nxt2.v)
            if k == 2 and ranked:
                dve_logits(oldest)
            if k == 2 and nxt:
                dve_values(nxt)
            if k == 3 and older and older.phase == 0:
                dve_stats(tiles(x_all, older), st2, res, NRES * older.v + 8)
            if k == 3 and ranked:
                dve_top(oldest, 1)
            if cur:
                dve_reduce(cur, k, 2)
                dve_split_max(cur, k)
            if k == 0 and placing:
                dve_place(first, 1)
            if k == 1 and nxt2 and nxt2.phase == 2:
                dve_combine(nxt2, 1)
            if k == 2 and older:
                dve_normalise(older)
            if k == 2 and ranked:
                dve_top(oldest, 0)
            if k == 3 and ranked:
                dve_top(oldest, 2)
            if k == 3 and placing:
                dve_place(first, 4)
            if k == 3 and placing:
                dve_place(first, 5)
            if k == 3 and older and older.phase == 0:
                need(dve, post_rstd, NRSTD * (older.v - 2) + 4)
                dve_moments(st2, mv2[:, older.par], res, NRES * older.v + 8)

        def pool_rstd(mv, r, s, base, last=1):
            alone(pool)
            nc.gpsimd.tensor_scalar(r, mv[:, :, 1], EPS, None, ALU.add).then_inc(s, 1)
            pool.wait_ge(s, base + 1)
            nc.gpsimd.tensor_tensor(r, r, power[:], ALU.pow).then_inc(s, last)

        def pool_select(i, g, u):
            pool.wait_ge(exp_done, unit(i, g, 2 * u))
            alone(pool)
            t = prob1[:, g % 2] if u == 0 else prob0[:, g % 2, :, 0:P]
            nc.gpsimd.affine_select(out=t, in_=t, compare_op=ALU.is_ge, fill=0.0, base=0,
                                    pattern=[[0, HG], [1, P]], channel_multiplier=-1).then_inc(sel_done, 1)

        def pool_rest(i):
            base = NSPLIT * i.v
            pool.wait_ge(qkf_sb, 4 * i.v + 4)
            need(pool, split, base)
            alone(pool)
            nc.gpsimd.tensor_tensor(rest[:], qkf[:], parts[:, i.par, :, 0], ALU.subtract).then_inc(split, 1)

        def pool_part(i):
            pool.wait_ge(split, NSPLIT * i.v + 2)
            alone(pool)
            nc.gpsimd.tensor_tensor(parts[:, i.par, :, 2], rest[:], parts[:, i.par, :, 1],
                                    ALU.subtract).then_inc(split, 1)

        def pool_send(i, n):
            t, rank = divmod(n, TOP)
            if n == 0:
                pool.wait_ge(placed, NPLACE * (i.v - B) + NPLACE)
                pool.wait_ge(hk_sb, i.v - B + 1)
                alone(pool)
            nc.gpsimd.indirect_dma_start(
                x_routed, bass.IndirectOffsetOnAxis(ap=x_at[:, i.par, t, rank:rank + 1], axis=0),
                hk[:, i.par, t], None).then_inc(x_sent[i.par], 16)

        def pool_fetch(i, n):
            u = i.v - 2 * B
            t, rank = divmod(n, TOP)
            if n == 0:
                pool.wait_ge(table, NTABLE)
                if isinstance(i.v, int) and i.b < 2:
                    for par in range(2):
                        pool.wait_ge(y_sent[par], 8 * JOBS)
                need(pool, combined, 4 * (u - 1))
                need(pool, y_fetch[i.par], fetched(i) - 16 * 2 * TOP)
                alone(pool)
                nc.gpsimd.tensor_copy(y_at[:, i.par], y_at_all[:, bass.ds(2 * i.b, 2)]).then_inc(fetch_at, 1)
                pool.wait_ge(fetch_at, u + 1)
                alone(pool)
            nc.gpsimd.indirect_dma_start(
                y_got[:, i.par, t, rank], None, y_routed,
                bass.IndirectOffsetOnAxis(ap=y_at[:, i.par, t, rank:rank + 1], axis=0))\
                .then_inc(y_fetch[i.par], 16)

        def pool_slot(step, k):
            nxt, nxt2, older, oldest, first = (item(step, d) for d in (1, 2, -2, -3, -4))
            ie, ge = group(step, k, 2)
            if k == 1 and nxt:
                pool_rest(nxt)
            if k == 2 and older:
                pool.wait_ge(res, summed(older) + 4)
                pool_rstd(post_mv[:, older.par], post_r[:, older.par], post_rstd, NRSTD * older.v,
                          1 if older.phase == 0 else NRSTD - 1)
            if k == 0 and oldest and oldest.phase == 0:
                pool.wait_ge(res, NRES * oldest.v + 12)
                pool_rstd(mv2[:, oldest.par], r2[:, oldest.par], post_rstd, NRSTD * oldest.v + 2)
            if ie:
                pool_select(ie, ge, 0)
            if k == 2 and nxt2:
                pool.wait_ge(pre_stats, NPRE * nxt2.v + 4)
                need(pool, xn_ok, 2 * (nxt2.v - 2) + 2)
                pool_rstd(pre_mv[:, nxt2.par], pre_r[:, nxt2.par], pre_rstd, 2 * nxt2.v)
            if k == 1 and nxt:
                pool_part(nxt)
            if ie:
                pool_select(ie, ge, 1)
            nxt3 = item(step, 3) if step_phase(step) == 2 else None
            if nxt3:
                pool_fetch(nxt3, k)
            sending = first if k == 3 else item(step, -5)
            if sending and sending.phase == 1:
                pool_send(sending, (k + 1) % NG)
            if k == 3 and oldest and oldest.phase == 1:
                pool.wait_ge(res, NRES * oldest.v + NRES)
                need(pool, x_sent[oldest.par], sent(oldest) - 16 * 2 * TOP)
                alone(pool)
                nc.gpsimd.tensor_copy(hk[:, oldest.par], hn[:, oldest.par]).then_inc(hk_sb, 1)

        def sp_stack(i, terms):
            if 0 in terms:
                sp.wait_ge(split, NSPLIT * i.v + NSPLIT)
                need(sp, sT_ps, 12 * (i.v - 2) + 12)
                alone(sp)
            qk = parts[:, i.par].rearrange("p w a t -> p (w a) t")
            for t in terms:
                a, b = TERM[t]
                sp.dma_start(stack[t * HD:(t + 1) * HD, i.par].rearrange("p h w t -> p (h w) t"),
                             qk[:, a:b + 4:b + 3 - a]).then_inc(stack_dma[i.par], 16)

        def sp_slot(step, k):
            nxt = item(step, 1)
            im, gm = group(step, k, 1)
            if k == 2 and nxt:
                sp_stack(nxt, range(0, 2))
            if im:
                sp.wait_ge(mT_sb, 4 * im.v + gm + 1)
                alone(sp)
                need(sp, sT_ps, 12 * (im.v - 2) + 3 * gm + 3)
                alone(sp)
                sp.dma_start(stack[SHIFT:P, im.par, HG * gm:HG * (gm + 1), 0],
                             mT[:, gm % 2, :]).then_inc(row_dma[gm % 2], 16)
            if k == 2 and nxt:
                sp_stack(nxt, range(2, 6))
            if k == 3 and nxt:
                sp_stack(nxt, range(6, TERMS))

        block = ctx.enter_context(nc.Block())
        RUNS = [(0, 2 * B), (2 * B, 3 * B)]
        CHOSEN, G0 = 12, 15
        NTABLE_JOBS, NTABLE = 18, 26

        def dve_tables():
            n = [0]

            def step(ins):
                n[0] += 1
                ins.then_inc(table, 1)
                dve.wait_ge(table, n[0])

            def view(shape):
                size = int(np.prod(shape[1:]))
                names = "abc"[:len(shape) - 1]
                spec = "p (" + " ".join(names) + ") -> p " + " ".join(names)
                return tb[:, 0:size].rearrange(spec, **dict(zip(names[1:], shape[2:])))

            dve.wait_ge(placed, NPLACE * B)
            t = view([P, E, MAXJ])
            step(nc.vector.tensor_copy(t, counts[:].unsqueeze(2).to_broadcast([P, E, MAXJ])))
            step(nc.vector.scalar_tensor_tensor(out=t, in0=t, scalar=1.0 / T,
                                                in1=iota_j[:, 0:MAXJ].unsqueeze(1).to_broadcast([P, E, MAXJ]),
                                                op0=ALU.mult, op1=ALU.is_gt))
            step(nc.vector.tensor_reduce(nj[:], t, AX.X, ALU.add))
            t = view([P, E, E])
            step(nc.vector.tensor_tensor(t, earlier[:], nj[:].unsqueeze(1).to_broadcast([P, E, E]), ALU.mult))
            step(nc.vector.tensor_reduce(js[:], t, AX.X, ALU.add))
            step(nc.vector.tensor_tensor(total[:], js[:, E - 1:E], nj[:, E - 1:E], ALU.add))
            t = view([P, JOBS, E])
            mask, start, row, spare, idle = (jt[:, i] for i in range(5))
            jobs_wide = iota_j[:].unsqueeze(2).to_broadcast([P, JOBS, E])
            starts = js[:].unsqueeze(1).to_broadcast([P, JOBS, E])
            step(nc.vector.tensor_tensor(t, jobs_wide, starts, ALU.is_ge))
            step(nc.vector.tensor_reduce(mask, t, AX.X, ALU.add))
            step(nc.vector.tensor_tensor(t, t, starts, ALU.mult))
            step(nc.vector.tensor_reduce(start, t, AX.X, ALU.max))
            step(nc.vector.tensor_scalar(job_e[:], mask, 1.0, None, ALU.subtract))
            step(nc.vector.tensor_tensor(row, iota_j[:], start, ALU.subtract))
            step(nc.vector.tensor_scalar(spare, mask, 1.0, float(REG), ALU.subtract, ALU.mult))
            step(nc.vector.scalar_tensor_tensor(out=row, in0=row, scalar=float(T), in1=spare, op0=ALU.mult,
                                                op1=ALU.add))
            step(nc.vector.tensor_tensor(idle, iota_j[:], total[:].to_broadcast([P, JOBS]), ALU.is_ge))
            step(nc.vector.tensor_scalar(row, row, float(E * REG), None, ALU.min))
            step(nc.vector.scalar_tensor_tensor(out=job_row[:], in0=idle, scalar=float(E * REG), in1=row,
                                                op0=ALU.mult, op1=ALU.max))
            step(nc.vector.scalar_tensor_tensor(out=pad_row[:], in0=iota_e[:], scalar=float(REG), in1=counts[:],
                                                op0=ALU.mult, op1=ALU.add))
            assert n[0] == NTABLE_JOBS
            t = view([P, NT * TOP, E])
            flat = [a[:].rearrange("p t r -> p (t r)") for a in (expert_all, place_all, y_at_all)]
            step(nc.vector.tensor_copy(t, flat[0].unsqueeze(2).to_broadcast([P, NT * TOP, E])))
            step(nc.vector.tensor_tensor(t, t, iota_e[:].unsqueeze(1).to_broadcast([P, NT * TOP, E]), ALU.is_equal))
            step(nc.vector.tensor_tensor(t, t, js[:].unsqueeze(1).to_broadcast([P, NT * TOP, E]), ALU.mult))
            step(nc.vector.tensor_reduce(flat[0], t, AX.X, ALU.add))
            step(nc.vector.scalar_tensor_tensor(out=flat[2], in0=flat[0], scalar=float(T), in1=flat[1],
                                                op0=ALU.mult, op1=ALU.add))
            dve.wait_ge(gate_a, 1)
            step(nc.vector.tensor_scalar(weight_all[:, :, 0], gap_all[:], 1.0, None, ALU.add))
            step(nc.vector.reciprocal(weight_all[:, :, 0], weight_all[:, :, 0]))
            step(nc.vector.tensor_tensor(weight_all[:, :, 1], gap_all[:], weight_all[:, :, 0], ALU.mult))
            assert n[0] == NTABLE

        def act_gap():
            act.wait_ge(top, NTOP * B)
            nc.scalar.activation(gap_all[:], gap_all[:], ACT.Exp).then_inc(gate_a, 1)

        def dve_gate():
            n = [0]
            N = B
            dve.wait_ge(lg_sb, 2 * B)
            nc.vector.tensor_tensor(gtmp[:, 0], hmean[:].unsqueeze(2).to_broadcast([P, B, E]),
                                    gw_s[:, 1:2].to_broadcast([P, B, E]), ALU.mult).then_inc(gate_p, 1)
            dve.wait_ge(gate_p, 2)
            lg = logits[:]
            nc.vector.scalar_tensor_tensor(out=lg, in0=pre_bank[:, 0:B * E].rearrange("p (b e) -> p b e", e=E),
                                           scalar=1.0 / T, in1=gb_s[:, 1:2].to_broadcast([P, B, E]),
                                           op0=ALU.mult, op1=ALU.add).then_inc(gate_p, 1)
            dve.wait_ge(gate_p, 3)

            def step(ins):
                n[0] += 1
                ins.then_inc(gate_v, 1)
                dve.wait_ge(gate_v, n[0])

            def wide(i):
                return gsm[:, i, 0:N].unsqueeze(2).to_broadcast([P, N, E])

            iota = iota_e[:].unsqueeze(1).to_broadcast([P, N, E])
            cur = lg
            for r in range(2):
                t, oh = gtmp[:, 1, 0:N], gtmp[:, 2, 0:N]
                step(nc.vector.tensor_reduce(gsm[:, r, 0:N], cur, AX.X, ALU.max))
                step(nc.vector.tensor_tensor(t, cur, wide(r), ALU.is_equal))
                step(nc.vector.scalar_tensor_tensor(out=t, in0=t, scalar=-100.0, in1=iota, op0=ALU.mult,
                                                    op1=ALU.add))
                step(nc.vector.tensor_reduce(gsm[:, 2 + r, 0:N], t, AX.X, ALU.min))
                if r == 0:
                    step(nc.vector.tensor_tensor(oh, t, wide(2 + r), ALU.is_equal))
                    step(nc.vector.scalar_tensor_tensor(out=gtmp[:, 3, 0:N], in0=oh, scalar=-3e38, in1=lg,
                                                        op0=ALU.mult, op1=ALU.add))
                    cur = gtmp[:, 3, 0:N]
            step(nc.vector.tensor_tensor(gsm[:, 4, 0:N], gsm[:, 1, 0:N], gsm[:, 0, 0:N], ALU.subtract))
            step(nc.vector.tensor_scalar(chosen[:], gsm[:, 2:4, 0:N], 100.0, None, ALU.add))
            assert n[0] == CHOSEN
            dve.wait_ge(gate_a, 2)
            step(nc.vector.tensor_scalar(gsm[:, 6, 0:N], gsm[:, 5, 0:N], 1.0, None, ALU.add))
            step(nc.vector.reciprocal(gsm[:, 6, 0:N], gsm[:, 6, 0:N]))
            step(nc.vector.tensor_tensor(gsm[:, 5, 0:N], gsm[:, 5, 0:N], gsm[:, 6, 0:N], ALU.mult))
            assert n[0] == G0

        def act_gate():
            act.wait_ge(gate_v, CHOSEN - 1)
            N = B
            nc.scalar.activation(gsm[:, 5, 0:N], gsm[:, 4, 0:N], ACT.Exp).then_inc(gate_a, 1)

        def pe_gate():
            pe.wait_ge(gate_p, 1)
            nc.tensor.matmul(pre_bank[:, 0:B * E], ones[:], gtmp[:, 0, 0:B].rearrange("p b e -> p (b e)"),
                             start=True, stop=True).then_inc(gate_p, 1)

        def pe_hidden(j, par, rows):
            pe.wait_ge(w1_got, j + 1)
            need(pe, gelu_done, FC * (j - 1))
            for c in range(FC):
                m = nc.tensor.matmul(bank[2 * par + c // 2][:, (c % 2) * T:(c % 2 + 1) * T],
                                     w1_job[:, par, c * P:(c + 1) * P], rows, start=True, stop=True)
                if c % 2:
                    m.then_inc(h_ps, 1)

        def pe_output(j, par):
            pe.wait_ge(w2_got, j + 1)
            pe.wait_ge(gelu_done, FC * j + FC)
            need(pe, acc, 2 * (j - 1))
            for t in range(2):
                for c in range(FC):
                    m = nc.tensor.matmul(bank[4 + par][:, t * P:(t + 1) * P],
                                         hid[:, par, c, t * P:(t + 1) * P], w2_job[:, par, c],
                                         start=(c == 0), stop=(c == FC - 1))
            m.then_inc(y_ps, 1)

        def act_gelu(j, par):
            need(act, y_ps, j - 1)
            act.wait_ge(b1_got, j + 1)
            for c in range(FC):
                if c % 2 == 0:
                    act.wait_ge(h_ps, 2 * j + c // 2 + 1)
                nc.scalar.activation(hid[:, par, c], bank[2 * par + c // 2][:, (c % 2) * T:(c % 2 + 1) * T],
                                     ACT.Gelu, bias=b1_job[:, par, c:c + 1]).then_inc(gelu_done, 1)

        def pool_w1(j, par, table_entry):
            e = nc.gpsimd.value_load(table_entry, min_val=0, max_val=E - 1)
            need(pool, h_ps, 2 * j - 2)
            alone(pool)
            nc.gpsimd.tensor_copy(w1_job[:, par:par + 1], w1_s[:, bass.ds(e, 1)]).then_inc(w1_got, 1)

        def dve_w2(layer, j, par, e):
            need(dve, y_ps, j - 1)
            need(dve, acc if layer == 0 else bias_add,
                 2 * j - 2 if layer == 0 else j - 1 - JOBS)
            alone(dve)
            nc.vector.tensor_copy(w2_job[:, par:par + 1], w2_s[:, bass.ds(e, 1)])
            nc.vector.tensor_copy(b2_job[:, par:par + 1], b2_all[:, bass.ds(e, 1)]).then_inc(w2_got, 1)

        def dve_b1(layer, j, par, e):
            need(dve, gelu_done, FC * (j - 1))
            alone(dve)
            nc.vector.tensor_copy(b1_job[:, par:par + 1], b1_s[:, layer, bass.ds(e, 1)]).then_inc(b1_got, 1)

        def expert_of(table_entry):
            return nc.vector.value_load(table_entry, min_val=0, max_val=E - 1)

        def run_jobs(eng, body, ahead=2):
            for j in range(2):
                body(j, j)
            with eng.Fori(2, JOBS - ahead - 1, 2) as j:
                for par in range(2):
                    body(j + par, par)
            for j in range(JOBS - ahead, JOBS):
                body(j, j % 2)

        def ahead(j, d):
            return not isinstance(j, int) or j + d < JOBS

        def times(j, par):
            return 8 * (j + (2 if par == 0 else 1))

        def pe_jobs():
            def rows_T(j, par):
                pe.wait_ge(x_got[par], times(j, par))
                need(pe, xjT_sb, j - 1)
                for t in range(2):
                    m = nc.tensor.transpose(bank[6 + par][:, t * P:(t + 1) * P], xj[:, par, t], ident[:])
                m.then_inc(xjT_ps, 1)

            def hidden(j, par):
                pe.wait_ge(xjT_sb, j + 1)
                pe_hidden(j, par, xjT[:, par])

            def body(j, par):
                if ahead(j, 2):
                    rows_T(j + 2, par)
                if ahead(j, 1):
                    hidden(j + 1, 1 - par)
                pe_output(j, par)

            pe.wait_ge(table, NTABLE_JOBS)
            rows_T(0, 0)
            rows_T(1, 1)
            hidden(0, 0)
            run_jobs(pe, body)

        def act_jobs():
            def rows_T(j, par):
                act.wait_ge(xjT_ps, j + 1)
                need(act, h_ps, 2 * j - 2)
                nc.scalar.activation(xjT[:, par], bank[6 + par][:, 0:T], ACT.Identity,
                                     scale=ln2_s[:, 0, 0:1], bias=ln2_s[:, 0, 1:2]).then_inc(xjT_sb, 1)

            def body(j, par):
                if ahead(j, 2):
                    rows_T(j + 2, par)
                if ahead(j, 1):
                    act_gelu(j + 1, 1 - par)

            rows_T(0, 0)
            rows_T(1, 1)
            act_gelu(0, 0)
            run_jobs(act, body)

        def entry(table, j):
            return table[0:1, j:j + 1] if isinstance(j, int) else table[0:1, bass.ds(j, 1)]

        def pool_jobs():
            def body(j, par):
                if ahead(j, 2):
                    pool_w1(j + 2, par, entry(job_e, j + 2))

            pool.wait_ge(expert_ld[0], 32 * E)
            pool.wait_ge(table, NTABLE_JOBS)
            for j in range(2):
                pool_w1(j, j, entry(job_e, j))
            run_jobs(pool, body)

        def dve_jobs():
            def body(j, par):
                if ahead(j, 2):
                    e = expert_of(entry(job_e, j + 2))
                    dve_b1(0, j + 2, par, e)
                dve.wait_ge(y_ps, j + 1)
                need(dve, y_sent[par], times(j, par) - 16)
                nc.vector.tensor_tensor(yj[:, par], bank[4 + par][:, 0:T].rearrange("p (t d) -> p t d", t=2),
                                        b2_job[:, par:par + 1].to_broadcast([P, 2, P]),
                                        ALU.add).then_inc(acc, 2)
                if ahead(j, 2):
                    dve_w2(0, j + 2, par, e)

            dve.wait_ge(expert_ld[0], 32 * E)
            for j in range(2):
                e = expert_of(entry(job_e, j))
                dve_b1(0, j, j, e)
                dve_w2(0, j, j, e)
            run_jobs(dve, body)

        def pads(eng, experts):
            for e in experts:
                row = eng.value_load(pad_row[0:1, e:e + 1], min_val=0, max_val=E * REG - T)
                eng.dma_start(x_routed[bass.ds(row, T)].rearrange("(t p) d -> p t d", p=P), zeros[:])\
                   .then_inc(pad_dma, 16)

        def sp_jobs():
            def load(j, par):
                row = nc.sync.value_load(entry(job_row, j), min_val=0, max_val=E * REG)
                need(sp, xjT_ps, j - 1)
                alone(sp)
                sp.dma_start(xj[:, par], x_routed[bass.ds(row, T)].rearrange("(t p) d -> p t d", p=P))\
                  .then_inc(x_got[par], 16)

            def body(j, par):
                if ahead(j, 4):
                    load(j + 4, par)
                sp.wait_ge(acc, 2 * j + 2)
                alone(sp)
                at = bass.ds(j * T, T)
                sp.dma_start(y_routed[at].rearrange("(t p) d -> p t d", p=P), yj[:, par]).then_inc(y_sent[par], 16)

            sp.wait_ge(table, NTABLE_JOBS)
            pads(sp, range(0, E // 2))
            sp.wait_ge(pad_dma, 16 * E)
            sp.wait_ge(zeros_dma, 16)
            for par in range(2):
                sp.wait_ge(x_sent[par], 8 * 2 * TOP * B)
            for j in range(4):
                load(j, j % 2)
            run_jobs(sp, body, 4)

        def pe_experts():
            def rows(b):
                return hT_all[:, bass.ds(b * T, T)]

            def body(b, last):
                j = JOBS + TOP * b
                pe_hidden(j + 1, 1, rows(b))
                pe_output(j, 0)
                if not last:
                    pe_hidden(j + 2, 0, rows(b + 1))
                pe_output(j + 1, 1)

            pe.wait_ge(hT_sb, 2 * B)
            pe.wait_ge(gate_v, CHOSEN)
            pe_hidden(JOBS, 0, rows(0))
            with pe.Fori(0, B - 1) as b:
                body(b, False)
            body(B - 1, True)

        def act_experts():
            def body(b):
                for r in range(TOP):
                    act_gelu(JOBS + TOP * b + r, r)
                if not isinstance(b, int) or b > 0:
                    act_final(b - 1)

            body(0)
            body(1)
            with act.Fori(2, B) as b:
                body(b)
            act_final(B - 1)

        def dve_final_stats(u):
            need(dve, fin_v, 4 * u)
            alone(dve)
            for j in range(2):
                f = f_all[:, bass.ds(2 * u + j, 1), :].rearrange("p a d -> p (a d)")
                nc.vector.bn_stats(st2[:, j], f).then_inc(fin_v, 1)

        def dve_final_moments(u):
            dve.wait_ge(fin_v, 4 * u + 2)
            need(dve, fin_p, u)
            alone(dve)
            for j in range(2):
                nc.vector.bn_aggr(mv2[:, 0, j], st2[:, j]).then_inc(fin_v, 1)

        def dve_final_scale(u):
            need(dve, fin_n, 2 * u)
            dve.wait_ge(fin_q, 2 * u + 2)
            nc.vector.scalar_tensor_tensor(out=r2[:, 1], in0=mv2[:, 0, :, 0], scalar=-1.0, in1=r2[:, 0],
                                           op0=ALU.mult, op1=ALU.mult).then_inc(fin_p, 1)

        def pool_final(u):
            pool.wait_ge(fin_v, 4 * u + 4)
            need(pool, fin_n, 2 * u)
            pool_rstd(mv2[:, 0], r2[:, 0], fin_q, 2 * u)

        def act_final(u):
            act.wait_ge(fin_p, u + 1)
            need(act, fin_x, u)
            alone(act)
            for j in range(2):
                f = f_all[:, bass.ds(2 * u + j, 1), :].rearrange("p a d -> p (a d)")
                nc.scalar.activation(hn[:, 0, j], f, ACT.Identity, scale=r2[:, 0, j:j + 1],
                                     bias=r2[:, 1, j:j + 1]).then_inc(fin_n, 1)

        def dve_final_x(u):
            dve.wait_ge(fin_n, 2 * u + 2)
            x = x_all[:, bass.ds(2 * u, 2), :]
            nc.vector.tensor_tensor(x, x, hn[:, 0], ALU.add).then_inc(fin_x, 1)

        def pool_experts():
            pool.wait_ge(gate_v, CHOSEN)
            pool.wait_ge(expert_ld[1], 32 * E)
            def body(b):
                for r in range(TOP):
                    pool_w1(JOBS + TOP * b + r, r, entry(chosen[:, r], b))
                if not isinstance(b, int) or b > 1:
                    pool_final(b - 2)

            for b in range(3):
                body(b)
            with pool.Fori(3, B) as b:
                body(b)
            for b in (B - 2, B - 1):
                pool_final(b)

        def dve_experts():
            def body(b, last):
                follow = not isinstance(b, int) or b > 0
                for r in range(TOP):
                    j = JOBS + TOP * b + r
                    weight = gsm[:, 6 - r, bass.ds(b, 1)]
                    if not last:
                        e = expert_of(chosen[0:1, r, bass.ds(b + 1, 1)])
                    need(dve, acc, 2 * j)
                    if follow:
                        (dve_final_stats, dve_final_scale)[r](b - 1)
                    dve.wait_ge(w2_got, j + 1)
                    pairs = f_all[:, bass.ds(2 * b, 2), :]
                    nc.vector.scalar_tensor_tensor(out=pairs, in0=b2_job[:, r:r + 1].to_broadcast([P, 2, P]),
                                                   scalar=weight, in1=pairs,
                                                   op0=ALU.mult, op1=ALU.add).then_inc(bias_add, 1)
                    if follow and r == 0:
                        dve_final_moments(b - 1)
                    if not last:
                        dve_b1(1, j + 2, r, e)
                    dve.wait_ge(bias_add, j - JOBS + 1)
                    dve.wait_ge(y_ps, j + 1)
                    for t in range(2):
                        f = f_all[:, bass.ds(2 * b + t, 1), :].rearrange("p a d -> p (a d)")
                        nc.vector.scalar_tensor_tensor(out=f, in0=bank[4 + r][:, t * P:(t + 1) * P],
                                                       scalar=weight, in1=f,
                                                       op0=ALU.mult, op1=ALU.add).then_inc(acc, 1)
                    if not last:
                        dve_w2(1, j + 2, r, e)
                if follow:
                    dve_final_x(b - 1)

            dve.wait_ge(bias_ld, 16)
            dve.wait_ge(expert_ld[1], 32 * E)
            for r in range(TOP):
                e = expert_of(chosen[0:1, r, 0:1])
                dve_b1(1, JOBS + r, r, e)
                dve_w2(1, JOBS + r, r, e)
            body(0, False)
            body(1, False)
            with dve.Fori(2, B - 1) as b:
                body(b, False)
            body(B - 1, True)
            dve.wait_ge(acc, 2 * (JOBS + TOP * B))
            for step in (dve_final_stats, dve_final_moments, dve_final_scale, dve_final_x):
                step(B - 1)

        @block.sync
        def _(_):
            sp.dma_start(x_all[:, 0:8], x_dram[:, 0:8]).then_inc(x_first, 16)
            for t, d in ((ln1_s, ln1), (wqk_s, w_qk), (wv_s, w_v)):
                sp.dma_start(t[:], d).then_inc(small_ld, 16)
            sp.dma_start(x_all[:, 8:NT], x_dram[:, 8:NT]).then_inc(x_rest, 16)
            sp.wait_ge(vconst_ok, 4)
            sp.dma_start(x_routed[E * REG:E * REG + T].rearrange("(t p) d -> p t d", p=P), zeros[:])\
              .then_inc(zeros_dma, 16)

            def filled():
                sp.wait_ge(qstack_ok, 1)
                sp.wait_ge(kstack_ok, 3)

            run_steps(sp, behind(sp_slot, -1, [filled]), *RUNS[0])
            sp_jobs()
            run_steps(sp, sp_slot, *RUNS[1])
            with sp.Fori(0, B) as b:
                sp.wait_ge(fin_x, b + 1)
                alone(sp)
                sp.dma_start(out_dram[:, bass.ds(2 * b, 2), :], x_all[:, bass.ds(2 * b, 2), :]).then_inc(out_dma, 16)
            sp.wait_ge(out_dma, 16 * B)

        @block.gpsimd
        def _(_):
            nc.gpsimd.memset(ident[:], 0.0).then_inc(const_ok, 1)
            nc.gpsimd.memset(maskneg[:], 0.0).then_inc(const_ok, 1)
            nc.gpsimd.memset(power[:], -0.5).then_inc(const_ok, 1)
            nc.gpsimd.memset(before[:], 1.0).then_inc(const_ok, 1)
            nc.gpsimd.memset(earlier[:], 1.0).then_inc(const_ok, 1)
            nc.gpsimd.iota(iota_j[:], pattern=[[1, JOBS]], base=0, channel_multiplier=0,
                           allow_small_or_imprecise_dtypes=True).then_inc(const_ok, 1)
            nc.gpsimd.iota(iota_e[:], pattern=[[1, E]], base=0, channel_multiplier=0,
                           allow_small_or_imprecise_dtypes=True).then_inc(const_ok, 1)
            pool.wait_ge(const_ok, 7)
            nc.gpsimd.affine_select(out=before[:], in_=before[:], compare_op=ALU.is_gt, fill=0.0, base=0,
                                    pattern=[[1, P]], channel_multiplier=-1).then_inc(const_ok, 1)
            nc.gpsimd.affine_select(out=earlier[:], in_=earlier[:], compare_op=ALU.is_gt, fill=0.0, base=0,
                                    pattern=[[1, E], [-1, E]], channel_multiplier=0).then_inc(const_ok, 1)
            nc.gpsimd.affine_select(out=ident[:], in_=ident[:], compare_op=ALU.not_equal, fill=1.0, base=0,
                                    pattern=[[-1, P]], channel_multiplier=1).then_inc(const_ok, 1)
            nc.gpsimd.affine_select(out=maskneg[:], in_=maskneg[:], compare_op=ALU.is_ge, fill=MASKED, base=0,
                                    pattern=[[0, HG], [-1, P]], channel_multiplier=1).then_inc(const_ok, 1)
            pool.wait_ge(const_ok, 11)
            nc.gpsimd.tensor_copy(identb[:], ident[:]).then_inc(const_ok, 1)

            def fill():
                nc.gpsimd.memset(stack[:, :, :, 0].bitcast(F32), 0.0).then_inc(qstack_ok, 1)

            run_steps(pool, behind(pool_slot, -1, [fill]), *RUNS[0])
            pool_jobs()
            run_steps(pool, pool_slot, *RUNS[1])
            pool_experts()

        @block.scalar
        def _(_):
            act.dma_start(bqk_s[:], b_qk).then_inc(small_ld, 16)
            act.dma_start(bv_s[:], b_v.partition_broadcast(P)).then_inc(small_ld, 16)
            for t, d in ((bo_s, b_o), (gb_s, gate_b), (b2_all, e_b2[:, 0])):
                act.dma_start(t[:], d.partition_broadcast(P)).then_inc(later_ld, 16)
            for t, d in ((wo_s, w_o), (ln2_s, ln2), (gw_s, gate_w), (b1_s, e_b1)):
                act.dma_start(t[:], d).then_inc(later_ld, 16)
            act.wait_ge(small_ld, SMALL)

            def load_experts(l):
                def piece(n):
                    e, which = divmod(n, 2)
                    if which == 0:
                        act.dma_start(w1_s[:, e], e_w1[l, e]).then_inc(expert_ld[l], 16)
                    else:
                        act.dma_start(w2_s[:, e], e_w2[l, e].rearrange("(c p) d -> p c d", p=P))\
                           .then_inc(expert_ld[l], 16)
                return [lambda n=n: piece(n) for n in range(2 * E)]

            first, *others = load_experts(0)

            def loaded():
                act.wait_ge(later_ld, LATER)
                first()

            run_steps(act, behind(act_slot, 0, [loaded, *others]), *RUNS[0])
            act_gap()
            act.wait_ge(table, NTABLE_JOBS)
            pads(act, range(E // 2, E))
            act_jobs()
            act.wait_ge(w1_got, JOBS)
            act.wait_ge(w2_got, JOBS)
            act.dma_start(b2_all[:], e_b2[:, 1].partition_broadcast(P)).then_inc(bias_ld, 16)
            run_steps(act, behind(act_slot, 2 * B, load_experts(1)), *RUNS[1])
            act_gate()
            act_experts()

        @block.vector
        def _(_):
            def fill():
                nc.vector.memset(vaug[:], 0.0).then_inc(kstack_ok, 1)
                dve.wait_ge(kstack_ok, 1)
                nc.vector.memset(vaug[:, :, :, :, HD:HD + 1], 1.0).then_inc(kstack_ok, 1)
                nc.vector.memset(stack[:, :, :, 1].bitcast(F32), TWO_ONES).then_inc(kstack_ok, 1)

            nc.vector.memset(ones[:], 1.0).then_inc(vconst_ok, 1)
            nc.vector.memset(onesb[:], 1.0).then_inc(vconst_ok, 1)
            nc.vector.memset(zeros[:], 0.0).then_inc(vconst_ok, 1)
            nc.vector.memset(counts[:], 0.0).then_inc(vconst_ok, 1)
            dve.wait_ge(small_ld, SMALL)
            dve.wait_ge(const_ok, 12)

            def loaded():
                fill()
                dve.wait_ge(later_ld, LATER)

            run_steps(dve, behind(dve_slot, -1, [loaded]), *RUNS[0])
            dve_tables()
            dve_jobs()
            run_steps(dve, dve_slot, *RUNS[1])
            dve_gate()
            dve_experts()

        @block.tensor
        def _(_):
            pe.wait_ge(const_ok, 12)
            pe.wait_ge(vconst_ok, 4)
            pe.wait_ge(small_ld, SMALL)
            run_steps(pe, behind(pe_slot, 0, [lambda: pe.wait_ge(later_ld, LATER)]), *RUNS[0])
            pe_jobs()
            run_steps(pe, pe_slot, *RUNS[1])
            pe_gate()
            pe_experts()



def kernel(**inputs):
    import concourse.bacc as bacc
    from concourse.bass_utils import run_bass_kernel_spmd

    a = {k: np.ascontiguousarray(v) for k, v in inputs.items()}
    f = {k[7:]: v for k, v in a.items() if k.startswith("L0_ffn_")}
    x, w_qkv, w_out = a["L0_attn_x"], a["L0_attn_w_qkv"], a["L0_attn_w_out"]
    zero, one = np.zeros(P, x.dtype), np.ones(P, x.dtype)

    def by_feature(w):
        return w.reshape(-1, H, HD).transpose(0, 2, 1).reshape(w.shape)

    def rows(vectors):
        return np.stack(vectors)

    def columns(vectors):
        return np.stack(vectors, axis=-1)

    qs = [w_qkv[:, 0:P], f["wq"][0], f["wq"][1]]
    ks = [w_qkv[:, P:2 * P], f["wk"][0], f["wk"][1]]
    vs = [w_qkv[:, 2 * P:], f["wv"][0], f["wv"][1]]
    os_ = [w_out, f["wo"][0], f["wo"][1]]
    arrays = {
        "x": x,
        "w_qk": np.stack([np.stack([by_feature(q), by_feature(k)], 1) for q, k in zip(qs, ks)], 1),
        "w_v": np.stack(vs, 1),
        "w_o": np.stack(os_, 1),
        "b_qk": np.stack([columns([by_feature(q[None])[0], by_feature(k[None])[0]])
                          for q, k in zip([zero, *f["bq"]], [zero, *f["bk"]])], 1),
        "b_v": rows([zero, *f["bv"]]),
        "b_o": rows([a["L0_attn_b_out"], *f["bo"]]),
        "ln1": np.stack([columns([w, b]) for w, b in zip([one, *f["ln1_w"]], [zero, *f["ln1_b"]])], 1),
        "ln2": np.stack([columns([w, b]) for w, b in zip(f["ln2_w"], f["ln2_b"])], 1),
        "gate_w": f["gate_w"].transpose(1, 0, 2),
        "gate_b": f["gate_b"],
        "e_w1": f["e_w1"],
        "e_b1": f["e_b1"].reshape(2, E, -1, P).transpose(3, 0, 1, 2),
        "e_w2": f["e_w2"],
        "e_b2": f["e_b2"].transpose(1, 0, 2),
    }
    arrays = {k: np.ascontiguousarray(v) for k, v in arrays.items()}
    nc = bacc.Bacc("TRN2", target_bir_lowering=False, num_devices=1)
    args = [nc.dram_tensor(k, v.shape, mybir.dt.from_np(v.dtype), kind="ExternalInput").ap()
            for k, v in arrays.items()]
    out = nc.dram_tensor("out", x.shape, F32, kind="ExternalOutput").ap()
    build(nc, *args, out)
    r = run_bass_kernel_spmd(nc, [arrays], core_ids=[0])
    return r.results[0]["out"]
```
